# Optimizing a Trainium2 kernel written in Bass

```python
import numpy as np
import jax
import jax.numpy as jnp

def _softmax(x, axis=-1):
    return jax.nn.softmax(x, axis=axis)

def _gelu(x):
    return jax.nn.gelu(x, approximate=True)

def _silu(x):
    return jax.nn.silu(x)

def _sigmoid(x):
    return jax.nn.sigmoid(x)

def _layernorm(x, axis=-1, eps=1e-05):
    m = jnp.mean(x, axis=axis, keepdims=True)
    v = jnp.var(x, axis=axis, keepdims=True)
    return (x - m) / jnp.sqrt(v + eps)

def _scatter_add(tgt, idx, src, axis=0):
    return tgt.at[idx].add(src)

def _segment_sum(src, seg, n):
    return jax.ops.segment_sum(src, seg, n)
kernel_name = 'mk_dlrm_tower_d1_rec_r8_42eb0e'

def setup_inputs(seed: int=0):
    np.random.seed(seed)
    _w = jnp.asarray

    def _rec_inputs():
        import jax
        import jax.numpy as jnp
        _tk = jax.random.key(seed)
        dense_ctx = jax.random.normal(jax.random.fold_in(_tk, 190), (512, 16), jnp.float32)
        ids = jnp.stack([jax.random.randint(jax.random.fold_in(_tk, 200 + f), (512,), 0, v, jnp.int32) for f, v in enumerate([125000, 12500, 1250, 1000, 1250, 1000, 125000, 1250, 1250, 125000, 125000, 12500, 1250, 125000, 1000, 125000, 1250, 1000, 1250, 1250, 1000, 1250, 1000, 125000, 125000, 1250, 1250, 125000, 1000, 125000, 1250, 1000, 1250, 1000, 1250, 125000, 125000, 1250, 1250])], axis=1)
        tbl_0 = 0.05 * jax.random.normal(jax.random.fold_in(_tk, 500 + 0), (125000, 16), jnp.float32)
        tbl_1 = 0.05 * jax.random.normal(jax.random.fold_in(_tk, 500 + 1), (12500, 16), jnp.float32)
        tbl_2 = 0.05 * jax.random.normal(jax.random.fold_in(_tk, 500 + 2), (1250, 16), jnp.float32)
        tbl_3 = 0.05 * jax.random.normal(jax.random.fold_in(_tk, 500 + 3), (1000, 16), jnp.float32)
        tbl_4 = 0.05 * jax.random.normal(jax.random.fold_in(_tk, 500 + 4), (1250, 16), jnp.float32)
        tbl_5 = 0.05 * jax.random.normal(jax.random.fold_in(_tk, 500 + 5), (1000, 16), jnp.float32)
        tbl_6 = 0.05 * jax.random.normal(jax.random.fold_in(_tk, 500 + 6), (125000, 16), jnp.float32)
        tbl_7 = 0.05 * jax.random.normal(jax.random.fold_in(_tk, 500 + 7), (1250, 16), jnp.float32)
        tbl_8 = 0.05 * jax.random.normal(jax.random.fold_in(_tk, 500 + 8), (1250, 16), jnp.float32)
        tbl_9 = 0.05 * jax.random.normal(jax.random.fold_in(_tk, 500 + 9), (125000, 16), jnp.float32)
        tbl_10 = 0.05 * jax.random.normal(jax.random.fold_in(_tk, 500 + 10), (125000, 16), jnp.float32)
        tbl_11 = 0.05 * jax.random.normal(jax.random.fold_in(_tk, 500 + 11), (12500, 16), jnp.float32)
        tbl_12 = 0.05 * jax.random.normal(jax.random.fold_in(_tk, 500 + 12), (1250, 16), jnp.float32)
        tbl_13 = 0.05 * jax.random.normal(jax.random.fold_in(_tk, 500 + 13), (125000, 16), jnp.float32)
        tbl_14 = 0.05 * jax.random.normal(jax.random.fold_in(_tk, 500 + 14), (1000, 16), jnp.float32)
        tbl_15 = 0.05 * jax.random.normal(jax.random.fold_in(_tk, 500 + 15), (125000, 16), jnp.float32)
        tbl_16 = 0.05 * jax.random.normal(jax.random.fold_in(_tk, 500 + 16), (1250, 16), jnp.float32)
        tbl_17 = 0.05 * jax.random.normal(jax.random.fold_in(_tk, 500 + 17), (1000, 16), jnp.float32)
        tbl_18 = 0.05 * jax.random.normal(jax.random.fold_in(_tk, 500 + 18), (1250, 16), jnp.float32)
        tbl_19 = 0.05 * jax.random.normal(jax.random.fold_in(_tk, 500 + 19), (1250, 16), jnp.float32)
        tbl_20 = 0.05 * jax.random.normal(jax.random.fold_in(_tk, 500 + 20), (1000, 16), jnp.float32)
        tbl_21 = 0.05 * jax.random.normal(jax.random.fold_in(_tk, 500 + 21), (1250, 16), jnp.float32)
        tbl_22 = 0.05 * jax.random.normal(jax.random.fold_in(_tk, 500 + 22), (1000, 16), jnp.float32)
        tbl_23 = 0.05 * jax.random.normal(jax.random.fold_in(_tk, 500 + 23), (125000, 16), jnp.float32)
        tbl_24 = 0.05 * jax.random.normal(jax.random.fold_in(_tk, 500 + 24), (125000, 16), jnp.float32)
        tbl_25 = 0.05 * jax.random.normal(jax.random.fold_in(_tk, 500 + 25), (1250, 16), jnp.float32)
        tbl_26 = 0.05 * jax.random.normal(jax.random.fold_in(_tk, 500 + 26), (1250, 16), jnp.float32)
        tbl_27 = 0.05 * jax.random.normal(jax.random.fold_in(_tk, 500 + 27), (125000, 16), jnp.float32)
        tbl_28 = 0.05 * jax.random.normal(jax.random.fold_in(_tk, 500 + 28), (1000, 16), jnp.float32)
        tbl_29 = 0.05 * jax.random.normal(jax.random.fold_in(_tk, 500 + 29), (125000, 16), jnp.float32)
        tbl_30 = 0.05 * jax.random.normal(jax.random.fold_in(_tk, 500 + 30), (1250, 16), jnp.float32)
        tbl_31 = 0.05 * jax.random.normal(jax.random.fold_in(_tk, 500 + 31), (1000, 16), jnp.float32)
        tbl_32 = 0.05 * jax.random.normal(jax.random.fold_in(_tk, 500 + 32), (1250, 16), jnp.float32)
        tbl_33 = 0.05 * jax.random.normal(jax.random.fold_in(_tk, 500 + 33), (1000, 16), jnp.float32)
        tbl_34 = 0.05 * jax.random.normal(jax.random.fold_in(_tk, 500 + 34), (1250, 16), jnp.float32)
        tbl_35 = 0.05 * jax.random.normal(jax.random.fold_in(_tk, 500 + 35), (125000, 16), jnp.float32)
        tbl_36 = 0.05 * jax.random.normal(jax.random.fold_in(_tk, 500 + 36), (125000, 16), jnp.float32)
        tbl_37 = 0.05 * jax.random.normal(jax.random.fold_in(_tk, 500 + 37), (1250, 16), jnp.float32)
        tbl_38 = 0.05 * jax.random.normal(jax.random.fold_in(_tk, 500 + 38), (1250, 16), jnp.float32)
        _rk = jax.random.fold_in(_tk, 7)
        W_top1 = 0.0606339 * jax.random.normal(jax.random.fold_in(_tk, 801), (272, 512), jnp.float32)
        W_top2 = 0.0441942 * jax.random.normal(jax.random.fold_in(_tk, 802), (512, 256), jnp.float32)
        W_top3 = 0.0625 * jax.random.normal(jax.random.fold_in(_tk, 803), (256, 1), jnp.float32)
        b_top1 = jnp.zeros((512,), jnp.float32)
        b_top2 = jnp.zeros((256,), jnp.float32)
        return (dense_ctx, ids, tbl_0, tbl_1, tbl_2, tbl_3, tbl_4, tbl_5, tbl_6, tbl_7, tbl_8, tbl_9, tbl_10, tbl_11, tbl_12, tbl_13, tbl_14, tbl_15, tbl_16, tbl_17, tbl_18, tbl_19, tbl_20, tbl_21, tbl_22, tbl_23, tbl_24, tbl_25, tbl_26, tbl_27, tbl_28, tbl_29, tbl_30, tbl_31, tbl_32, tbl_33, tbl_34, tbl_35, tbl_36, tbl_37, tbl_38, W_top1, b_top1, W_top2, b_top2, W_top3)
    dense_ctx, ids, tbl_0, tbl_1, tbl_2, tbl_3, tbl_4, tbl_5, tbl_6, tbl_7, tbl_8, tbl_9, tbl_10, tbl_11, tbl_12, tbl_13, tbl_14, tbl_15, tbl_16, tbl_17, tbl_18, tbl_19, tbl_20, tbl_21, tbl_22, tbl_23, tbl_24, tbl_25, tbl_26, tbl_27, tbl_28, tbl_29, tbl_30, tbl_31, tbl_32, tbl_33, tbl_34, tbl_35, tbl_36, tbl_37, tbl_38, W_top1, b_top1, W_top2, b_top2, W_top3 = _rec_inputs()

    def _L0_rec_setup():
        import jax, jax.numpy as jnp
        import numpy as np
        key = jax.random.key(seed)
        k1, k2, k3 = jax.random.split(key, 3)
        B, M, D = (512, 39, 16)
        H = [128, 128]
        x = jax.random.normal(k1, (B, M, D), dtype=jnp.float32)
        W0 = jax.random.normal(k2, (1, M * M, H[0]), dtype=jnp.float32) * 0.05
        W1 = jax.random.normal(k3, (1, M * H[0], H[1]), dtype=jnp.float32) * 0.05
        return {'x': x, 'W0': W0, 'W1': W1}
    _L0_rec_all = _L0_rec_setup()
    _L0_rec_in = {k: v for k, v in _L0_rec_all.items() if k in ('W0', 'W1')}
    del _L0_rec_all
    return {'dense_ctx': dense_ctx, 'ids': ids, 'tbl_0': tbl_0, 'tbl_1': tbl_1, 'tbl_2': tbl_2, 'tbl_3': tbl_3, 'tbl_4': tbl_4, 'tbl_5': tbl_5, 'tbl_6': tbl_6, 'tbl_7': tbl_7, 'tbl_8': tbl_8, 'tbl_9': tbl_9, 'tbl_10': tbl_10, 'tbl_11': tbl_11, 'tbl_12': tbl_12, 'tbl_13': tbl_13, 'tbl_14': tbl_14, 'tbl_15': tbl_15, 'tbl_16': tbl_16, 'tbl_17': tbl_17, 'tbl_18': tbl_18, 'tbl_19': tbl_19, 'tbl_20': tbl_20, 'tbl_21': tbl_21, 'tbl_22': tbl_22, 'tbl_23': tbl_23, 'tbl_24': tbl_24, 'tbl_25': tbl_25, 'tbl_26': tbl_26, 'tbl_27': tbl_27, 'tbl_28': tbl_28, 'tbl_29': tbl_29, 'tbl_30': tbl_30, 'tbl_31': tbl_31, 'tbl_32': tbl_32, 'tbl_33': tbl_33, 'tbl_34': tbl_34, 'tbl_35': tbl_35, 'tbl_36': tbl_36, 'tbl_37': tbl_37, 'tbl_38': tbl_38, 'W_top1': W_top1, 'b_top1': b_top1, 'W_top2': W_top2, 'b_top2': b_top2, 'W_top3': W_top3, 'L0_rec_W0': _L0_rec_in['W0'], 'L0_rec_W1': _L0_rec_in['W1']}

def reference(dense_ctx, ids, tbl_0, tbl_1, tbl_2, tbl_3, tbl_4, tbl_5, tbl_6, tbl_7, tbl_8, tbl_9, tbl_10, tbl_11, tbl_12, tbl_13, tbl_14, tbl_15, tbl_16, tbl_17, tbl_18, tbl_19, tbl_20, tbl_21, tbl_22, tbl_23, tbl_24, tbl_25, tbl_26, tbl_27, tbl_28, tbl_29, tbl_30, tbl_31, tbl_32, tbl_33, tbl_34, tbl_35, tbl_36, tbl_37, tbl_38, W_top1, b_top1, W_top2, b_top2, W_top3, L0_rec_W0, L0_rec_W1):
    import jax
    import jax.numpy as jnp

    def _L0_rec_ref(x, W0, W1):
        import jax, jax.numpy as jnp
        import numpy as np
        m = x.shape[1]
        x0 = x
        xk = x
        outs = []
        for W in (W0, W1):
            Hk = xk.shape[1]
            Hn = W.shape[-1]
            Wr = W.reshape(m, Hk, Hn)
            xk = jnp.einsum('bid,bjd,ijh->bhd', x0, xk, Wr)
            outs.append(xk)
        result = jnp.concatenate(outs, axis=1)
        return jnp.sum(result, axis=-1)
    e = jnp.stack([tbl_0[ids[:, 0]], tbl_1[ids[:, 1]], tbl_2[ids[:, 2]], tbl_3[ids[:, 3]], tbl_4[ids[:, 4]], tbl_5[ids[:, 5]], tbl_6[ids[:, 6]], tbl_7[ids[:, 7]], tbl_8[ids[:, 8]], tbl_9[ids[:, 9]], tbl_10[ids[:, 10]], tbl_11[ids[:, 11]], tbl_12[ids[:, 12]], tbl_13[ids[:, 13]], tbl_14[ids[:, 14]], tbl_15[ids[:, 15]], tbl_16[ids[:, 16]], tbl_17[ids[:, 17]], tbl_18[ids[:, 18]], tbl_19[ids[:, 19]], tbl_20[ids[:, 20]], tbl_21[ids[:, 21]], tbl_22[ids[:, 22]], tbl_23[ids[:, 23]], tbl_24[ids[:, 24]], tbl_25[ids[:, 25]], tbl_26[ids[:, 26]], tbl_27[ids[:, 27]], tbl_28[ids[:, 28]], tbl_29[ids[:, 29]], tbl_30[ids[:, 30]], tbl_31[ids[:, 31]], tbl_32[ids[:, 32]], tbl_33[ids[:, 33]], tbl_34[ids[:, 34]], tbl_35[ids[:, 35]], tbl_36[ids[:, 36]], tbl_37[ids[:, 37]], tbl_38[ids[:, 38]]], axis=1)
    z = _L0_rec_ref(e, L0_rec_W0, L0_rec_W1)
    z = z.reshape(z.shape[0], -1)
    h = jnp.concatenate([z, dense_ctx], axis=1)
    h = jnp.maximum(h @ W_top1 + b_top1, 0.0)
    h = jnp.maximum(h @ W_top2 + b_top2, 0.0)
    y = h @ W_top3
    return y

_drawn_inputs = setup_inputs


def setup_inputs(seed=0):
    import zlib

    import numpy as np

    out = dict(_drawn_inputs(seed))
    spreads = {'b_top1': (0.0, 0.1), 'b_top2': (0.0, 0.1)}
    factors = {'tbl_0': 4.952,
     'tbl_1': 5.46,
     'tbl_2': 4.799,
     'tbl_3': 5.33,
     'tbl_4': 5.01,
     'tbl_5': 5.335,
     'tbl_6': 5.219,
     'tbl_7': 5.224,
     'tbl_8': 5.135,
     'tbl_9': 4.69,
     'tbl_10': 5.469,
     'tbl_11': 4.81,
     'tbl_12': 4.678,
     'tbl_13': 4.905,
     'tbl_14': 4.988,
     'tbl_15': 5.028,
     'tbl_16': 5.56,
     'tbl_17': 4.668,
     'tbl_18': 5.36,
     'tbl_19': 5.356,
     'tbl_20': 5.082,
     'tbl_21': 5.15,
     'tbl_22': 4.708,
     'tbl_23': 4.992,
     'tbl_24': 4.753,
     'tbl_25': 4.851,
     'tbl_26': 5.333,
     'tbl_27': 5.326,
     'tbl_28': 4.971,
     'tbl_29': 5.028,
     'tbl_30': 5.233,
     'tbl_31': 4.594,
     'tbl_32': 5.155,
     'tbl_33': 4.766,
     'tbl_34': 4.972,
     'tbl_35': 4.916,
     'tbl_36': 5.043,
     'tbl_37': 5.077,
     'tbl_38': 5.071,
     'L0_rec_W1': 5.563}
    for name, (base, spread) in spreads.items():
        noise = np.random.default_rng([zlib.crc32(name.encode()), seed]).standard_normal(out[name].shape)
        drawn = base * np.exp(spread * noise) if base else spread * noise
        out[name] = jnp.asarray(drawn.astype(out[name].dtype))
    for name, factor in factors.items():
        out[name] = (out[name] * factor).astype(out[name].dtype)
    return out
```

```python
from contextlib import ExitStack

import concourse.bass as bass
from concourse import mybir

F32 = mybir.dt.float32
BF16 = mybir.dt.bfloat16
I32 = mybir.dt.int32
ACT = mybir.ActivationFunctionType
ALU = mybir.AluOpType

B, M, D = 512, 39, 16
H = 128
CH = 128
NCH = B // CH
BB = 32
NB = CH // BB
GB = 8
NG = BB // GB
COLS = BB * D
P3 = 3 * M
NT = 7
ROWS = [P3] * 6 + [2 * M]
MO = M + 1
GC = MO * GB
DENSE, F1, F2 = 16, 512, 256
M1, M2 = F1 // 128, F2 // 128


def build_tower(nc, ids, tables, pair_w_a, pair_w_b, select, w1, w_top1, w_dense, b_top1, w_top2, b_top2, w_top3,
                dense_t, ident_b, own_row, y):
    with ExitStack() as ctx:
        def sb(name, shape, dt=F32):
            return ctx.enter_context(nc.sbuf_tensor(name, shape, dt))

        def bank(name):
            return ctx.enter_context(nc.psum_tensor(name, [128, 512], F32))

        def sem(name):
            return ctx.enter_context(nc.semaphore(name))

        ids_sb = sb("ids_sb", [128, NCH * M], I32)
        wa = sb("wa", [P3, NT, H])
        wb = sb("wb", [P3, NT, H])
        pair_w = sb("pair_w", [P3, NT, H])
        sel = sb("sel", [P3, NT + 1, P3], BF16)
        w1_sb = sb("w1_sb", [128, M, H])
        wt1 = sb("wt1", [128, 2, F1])
        wtd = sb("wtd", [DENSE, F1])
        bt1 = sb("bt1", [128, M1])
        wt2 = sb("wt2", [128, M1, F2])
        bt2 = sb("bt2", [128, M2])
        wt3 = sb("wt3", [128, M2])
        dense_sb = sb("dense_sb", [DENSE, B])
        idb = sb("idb", [128, 128], BF16)
        own = sb("own", [128, GB])
        emb = sb("emb", [128, NCH * M * D])
        rest = sb("rest", [128, M * D])
        parts = sb("parts", [128, 3, M, D], BF16)
        x3 = sb("x3", [P3, CH, D], BF16)
        xrep = sb("xrep", [P3, 2, COLS])
        prod = sb("prod", [P3, 2, NT, COLS])
        x1 = sb("x1", [128, 2, NG * H])
        xblk = sb("xblk", [128, 2, NG, MO, GB])
        g_sb = sb("g_sb", [128, MO, CH])
        z2 = sb("z2", [128, CH])
        h1 = sb("h1", [128, M1, CH])
        h2 = sb("h2", [128, M2, CH])
        y_sb = sb("y_sb", [1, B])

        pair_bank = [bank("pair_bank0"), bank("pair_bank1")]
        turn_bank = bank("turn_bank")
        x1_bank = [bank("x1_bank0"), bank("x1_bank1")]
        g_bank = [bank("g_bank0"), bank("g_bank1")]
        misc_bank = bank("misc_bank")

        ids_in = sem("ids_in")
        pair_w_in = sem("pair_w_in")
        small_in = sem("small_in")
        w1_in = sem("w1_in")
        mlp_in = sem("mlp_in")
        gathered = [sem(f"gathered{c}") for c in range(NCH)]
        chunk_in = sem("chunk_in")
        split_step = sem("split_step")
        turned = sem("turned")
        x3_a = sem("x3_a")
        x3_b = sem("x3_b")
        rep_sel = sem("rep_sel")
        rep_done = sem("rep_done")
        pair_sel = sem("pair_sel")
        prod_done = sem("prod_done")
        pair_w_done = sem("pair_w_done")
        ones_done = sem("ones_done")
        xt_done = sem("xt_done")
        xblk_done = sem("xblk_done")
        x1_mm = sem("x1_mm")
        x1_done = sem("x1_done")
        g_mm = sem("g_mm")
        g_act = sem("g_act")
        g_dve = sem("g_dve")
        z2_mm = sem("z2_mm")
        z2_done = sem("z2_done")
        h1_mm = sem("h1_mm")
        h1_done = sem("h1_done")
        h2_mm = sem("h2_mm")
        h2_done = sem("h2_done")
        y_mm = sem("y_mm")
        mlp_through = sem("mlp_through")
        y_out = sem("y_out")

        def wait(eng, s, value):
            if not isinstance(value, int) or value > 0:
                eng.wait_ge(s, value)

        block = ctx.enter_context(nc.Block())

        @block.sync
        def _(sp):
            sp.dma_start(ids_sb[:, :], ids).then_inc(ids_in, 16)
            sp.dma_start(wa[:, :, :], pair_w_a).then_inc(pair_w_in, 16)
            sp.dma_start(wb[:, :, :], pair_w_b).then_inc(pair_w_in, 16)
            sp.dma_start(sel[:, :, :], select).then_inc(small_in, 16)
            sp.dma_start(idb[:, :], ident_b).then_inc(small_in, 16)
            sp.dma_start(own[:, :], own_row).then_inc(small_in, 16)
            sp.dma_start(w1_sb[:, :, :], w1.rearrange("(i j) h -> j i h", i=M)).then_inc(w1_in, 16)
            sp.dma_start(wt1[:, :, :], w_top1.rearrange("(k p) n -> p k n", p=128)).then_inc(mlp_in, 16)
            sp.dma_start(wtd[:, :], w_dense).then_inc(mlp_in, 16)
            sp.dma_start(bt1[:, :], b_top1).then_inc(mlp_in, 16)
            sp.dma_start(wt2[:, :, :], w_top2.rearrange("(k p) n -> p k n", p=128)).then_inc(mlp_in, 16)
            sp.dma_start(bt2[:, :], b_top2).then_inc(mlp_in, 16)
            sp.dma_start(wt3[:, :], w_top3).then_inc(mlp_in, 16)
            sp.dma_start(dense_sb[:, :], dense_t).then_inc(mlp_in, 16)
            for c in range(NCH):
                sp.wait_ge(gathered[c], 16 * M)
                sp.sem_inc(chunk_in, 1)
            sp.wait_ge(mlp_through, NCH + 1)
            sp.dma_start(y, y_sb[:, :]).then_inc(y_out, 16)
            sp.wait_ge(y_out, 16)

        @block.gpsimd
        def _(pool):
            pool.wait_ge(ids_in, 16)
            for c in range(NCH):
                for f in range(M):
                    at = (c * M + f) * D
                    pool.indirect_dma_start(
                        out=emb[:, at:at + D], out_offset=None, in_=tables[f],
                        in_offset=bass.IndirectOffsetOnAxis(ap=ids_sb[:, c * M + f:c * M + f + 1], axis=0),
                    ).then_inc(gathered[c], 16)

        @block.tensor
        def _(pe):
            def turn(c):
                pe.wait_ge(split_step, 4 * c + 4)
                wait(pe, mlp_through, c)
                for half, to in ((0, turn_bank), (1, misc_bank)):
                    if half:
                        wait(pe, xblk_done, NB * c)
                    out = to[0:P3, :].bitcast(BF16).rearrange("p (d b) -> p d b", b=CH)
                    for d in range(D // 2):
                        mm = pe.transpose(out[:, d, :], parts[:, :, :, half * D // 2 + d].rearrange("b q i -> b (q i)"),
                                          idb[:, :])
                    mm.then_inc(turned, 1)

            def select_rep(c, j):
                k = NB * c + j
                wait(pe, prod_done, NT * k - 1)
                pe.matmul(pair_bank[0][0:P3, :], sel[:, NT, :], x3[:, j * BB:(j + 1) * BB, :],
                          start=True, stop=True).then_inc(rep_sel, 1)

            def select_pair(c, j, t):
                k = NB * c + j
                if t == 0:
                    wait(pe, prod_done, NT * k)
                elif t == 1:
                    pe.wait_ge(rep_done, k + 1)
                else:
                    wait(pe, prod_done, NT * k + t - 1)
                pe.matmul(pair_bank[(t + 1) % 2][0:ROWS[t], :], sel[:, t, 0:ROWS[t]], x3[:, j * BB:(j + 1) * BB, :],
                          start=True, stop=True).then_inc(pair_sel, 1)

            def turn_x(c, j):
                k = NB * c + j
                wait(pe, xblk_done, k)
                if j == 1:
                    wait(pe, z2_done, c)
                for g in range(NG):
                    col = (j * NG + g) * GB
                    mm = pe.matmul(misc_bank[:, g * MO:g * MO + M], x3[:, col:col + GB, :], sel[:, NT, 0:M],
                                   start=True, stop=True)
                mm.then_inc(xt_done, 1)

            def layer1(c, j, g):
                k = NB * c + j
                if g == 0:
                    pe.wait_ge(prod_done, NT * (k + 1))
                    wait(pe, x1_done, k - 1)
                for t in range(NT):
                    mm = pe.matmul(x1_bank[j % 2][:, g * H:(g + 1) * H], prod[0:ROWS[t], j % 2, t, g * 128:(g + 1) * 128],
                                   pair_w[0:ROWS[t], t, :], start=(t == 0), stop=(t == NT - 1))
                if g == NG - 1:
                    mm.then_inc(x1_mm, 1)

            def contract_d(c, j, g):
                k = NB * c + j
                if g == 0:
                    pe.wait_ge(x1_done, k + 1)
                    pe.wait_ge(xblk_done, k + 1)
                wait(pe, g_dve if g % 2 else g_act, 2 * k + g // 2)
                pe.matmul(g_bank[g % 2][:, 0:GC], x1[:, j % 2, g * H:(g + 1) * H],
                          xblk[:, j % 2, g, :, :].rearrange("p i b -> p (i b)"), start=True, stop=True).then_inc(g_mm, 1)

            def layer2(c, i0, i1):
                if i0 == 0:
                    pe.wait_ge(g_act, 2 * NB * (c + 1))
                    pe.wait_ge(g_dve, 2 * NB * (c + 1))
                    if not isinstance(c, int):
                        pe.wait_ge(xblk_done, NB * (c + 1) + 1)
                for i in range(i0, i1):
                    mm = pe.matmul(misc_bank[:, 384:384 + CH], w1_sb[:, i, :], g_sb[:, i, :], start=(i == 0), stop=(i == M - 1))
                if i1 == M:
                    mm.then_inc(z2_mm, 1)

            def mlp1(c):
                pe.wait_ge(z2_done, c + 1)
                for m in range(M1):
                    out = turn_bank[:, m * CH:(m + 1) * CH]
                    cols = slice(m * 128, (m + 1) * 128)
                    pe.matmul(out, wt1[:, 0, cols], g_sb[:, M, :], start=True, stop=False)
                    pe.matmul(out, wt1[:, 1, cols], z2[:, :], start=False, stop=False)
                    mm = pe.matmul(out, wtd[:, cols], dense_sb[:, bass.ds(c * CH, CH)], start=False, stop=True)
                mm.then_inc(h1_mm, 1)

            def mlp2(c):
                pe.wait_ge(h1_done, M1 * (c + 1))
                for m in range(M2):
                    for k in range(M1):
                        mm = pe.matmul(turn_bank[:, m * CH:(m + 1) * CH], wt2[:, k, m * 128:(m + 1) * 128], h1[:, k, :],
                                       start=(k == 0), stop=(k == M1 - 1))
                mm.then_inc(h2_mm, 1)

            def mlp3(c):
                pe.wait_ge(h2_done, M2 * (c + 1))
                for k in range(M2):
                    mm = pe.matmul(turn_bank[0:1, 0:CH], wt3[:, k:k + 1], h2[:, k, :], start=(k == 0), stop=(k == M2 - 1))
                mm.then_inc(y_mm, 1)

            def later_blocks(c, has_previous):
                for j in range(1, NB):
                    select_rep(c, j)
                    select_pair(c, j, 0)
                    layer1(c, j - 1, 0)
                    select_pair(c, j, 1)
                    layer1(c, j - 1, 1)
                    select_pair(c, j, 2)
                    layer1(c, j - 1, 2)
                    select_pair(c, j, 3)
                    layer1(c, j - 1, 3)
                    select_pair(c, j, 4)
                    if j >= 2:
                        contract_d(c, j - 2, 0)
                    select_pair(c, j, 5)
                    if j >= 2:
                        contract_d(c, j - 2, 1)
                    select_pair(c, j, 6)
                    if j >= 2:
                        contract_d(c, j - 2, 2)
                        contract_d(c, j - 2, 3)
                    turn_x(c, j)
                    if has_previous:
                        (None, mlp1, mlp2, mlp3)[j](c - 1)

            pe.wait_ge(small_in, 48)
            turn(0)
            pe.wait_ge(x3_a, 1)
            pe.wait_ge(x3_b, 1)
            select_rep(0, 0)
            for t in range(NT):
                select_pair(0, 0, t)
            turn_x(0, 0)
            pe.wait_ge(pair_w_done, 1)
            pe.wait_ge(ones_done, 1)
            later_blocks(0, False)
            pe.wait_ge(w1_in, 16)
            pe.wait_ge(mlp_in, 16 * 7)
            with pe.Fori(1, NCH) as c:
                layer1(c - 1, 3, 0)
                layer1(c - 1, 3, 1)
                turn(c)
                layer1(c - 1, 3, 2)
                layer1(c - 1, 3, 3)
                contract_d(c - 1, 2, 0)
                contract_d(c - 1, 2, 1)
                contract_d(c - 1, 2, 2)
                contract_d(c - 1, 2, 3)
                pe.wait_ge(x3_a, c + 1)
                pe.wait_ge(x3_b, c + 1)
                select_rep(c, 0)
                select_pair(c, 0, 0)
                for g in range(NG):
                    contract_d(c - 1, 3, g)
                    if g < 2:
                        select_pair(c, 0, g + 1)
                turn_x(c, 0)
                for n in range(4):
                    layer2(c - 1, n * 10, min(n * 10 + 10, M))
                    select_pair(c, 0, n + 3)
                later_blocks(c, True)
            c = NCH - 1
            for g in range(NG):
                layer1(c, 3, g)
            for g in range(NG):
                contract_d(c, 2, g)
            for g in range(NG):
                contract_d(c, 3, g)
            layer2(c, 0, M)
            mlp1(c)
            mlp2(c)
            mlp3(c)

        @block.vector
        def _(dve):
            def split(c):
                flat = parts[:, :, :, :].rearrange("b q i d -> b q (i d)")
                dve.wait_ge(chunk_in, c + 1)
                dve.tensor_copy(flat[:, 0, :], emb[:, bass.ds(c * M * D, M * D)]).then_inc(split_step, 1)
                dve.wait_ge(split_step, 4 * c + 1)
                dve.tensor_tensor(rest[:, :], emb[:, bass.ds(c * M * D, M * D)], flat[:, 0, :],
                                  ALU.subtract).then_inc(split_step, 1)
                dve.wait_ge(split_step, 4 * c + 2)
                dve.tensor_copy(flat[:, 1, :], rest[:, :]).then_inc(split_step, 1)
                dve.wait_ge(split_step, 4 * c + 3)
                dve.tensor_tensor(flat[:, 2, :], rest[:, :], flat[:, 1, :], ALU.subtract).then_inc(split_step, 1)

            def keep_turned(c):
                dve.wait_ge(turned, 2 * c + 1)
                dve.tensor_copy(x3[:, :, 0:D // 2].rearrange("p b d -> p d b"),
                                turn_bank[0:P3, :].bitcast(BF16).rearrange("p (d b) -> p d b", b=CH)).then_inc(x3_a, 1)

            def multiply(c, j, t):
                k = NB * c + j
                if t == 0:
                    dve.wait_ge(rep_done, k + 1)
                    wait(dve, x1_mm, k - 1)
                dve.wait_ge(pair_sel, NT * k + t + 1)
                dve.tensor_tensor(prod[0:ROWS[t], j % 2, t, :], pair_bank[(t + 1) % 2][0:ROWS[t], :],
                                  xrep[0:ROWS[t], j % 2, :], ALU.mult).then_inc(prod_done, 1)

            def spread(c, j):
                k = NB * c + j
                dve.wait_ge(xt_done, k + 1)
                wait(dve, g_mm, NG * (k - 1))
                dve.tensor_tensor(
                    xblk[:, j % 2, :, 0:M, :],
                    misc_bank[:, 0:NG * MO].rearrange("p (g i) -> p g i", g=NG)[:, :, 0:M].unsqueeze(3).to_broadcast([128, NG, M, GB]),
                    own[:, :].unsqueeze(1).unsqueeze(1).to_broadcast([128, NG, M, GB]),
                    ALU.mult).then_inc(xblk_done, 1)

            def keep_g(c, j, g):
                k = NB * c + j
                dve.wait_ge(g_mm, NG * k + g + 1)
                dve.tensor_copy(g_sb[:, :, (j * NG + g) * GB:(j * NG + g + 1) * GB],
                                g_bank[g % 2][:, 0:GC].rearrange("p (i b) -> p i b", b=GB)).then_inc(g_dve, 1)

            def later_blocks(c):
                for j in range(1, NB):
                    multiply(c, j, 0)
                    multiply(c, j, 1)
                    for t in range(2, NT - 1):
                        multiply(c, j, t)
                    if j >= 2:
                        keep_g(c, j - 2, 1)
                    multiply(c, j, NT - 1)
                    if j >= 2:
                        keep_g(c, j - 2, 3)
                    spread(c, j)

            dve.wait_ge(pair_w_in, 32)
            dve.tensor_tensor(pair_w[:, :, :], wa[:, :, :], wb[:, :, :], ALU.add).then_inc(pair_w_done, 1)
            dve.wait_ge(small_in, 48)
            dve.tensor_copy(xblk[:, :, :, M, :].rearrange("p a g b -> p (a g) b"),
                            own[:, :].unsqueeze(1).to_broadcast([128, 2 * NG, GB])).then_inc(ones_done, 1)
            split(0)
            keep_turned(0)
            for t in range(NT):
                multiply(0, 0, t)
            spread(0, 0)
            later_blocks(0)
            with dve.Fori(1, NCH) as c:
                split(c)
                keep_turned(c)
                keep_g(c - 1, 2, 1)
                keep_g(c - 1, 2, 3)
                multiply(c, 0, 0)
                multiply(c, 0, 1)
                keep_g(c - 1, 3, 1)
                multiply(c, 0, 2)
                keep_g(c - 1, 3, 3)
                spread(c, 0)
                for t in range(3, NT):
                    multiply(c, 0, t)
                later_blocks(c)
            c = NCH - 1
            keep_g(c, 2, 1)
            keep_g(c, 2, 3)
            keep_g(c, 3, 1)
            keep_g(c, 3, 3)

        @block.scalar
        def _(act):
            def keep_turned(c):
                act.wait_ge(turned, 2 * c + 2)
                act.activation(x3[:, :, D // 2:D].rearrange("p b d -> p d b"),
                               misc_bank[0:P3, :].bitcast(BF16).rearrange("p (d b) -> p d b", b=CH),
                               ACT.Copy).then_inc(x3_b, 1)

            def keep_rep(c, j):
                k = NB * c + j
                act.wait_ge(rep_sel, k + 1)
                wait(act, prod_done, NT * (k - 1))
                act.activation(xrep[:, j % 2, :], pair_bank[0][0:P3, :], ACT.Copy).then_inc(rep_done, 1)

            def keep_x1(c, j):
                k = NB * c + j
                act.wait_ge(x1_mm, k + 1)
                wait(act, g_mm, NG * (k - 1))
                act.activation(x1[:, j % 2, :], x1_bank[j % 2][:, :], ACT.Copy).then_inc(x1_done, 1)

            def keep_g(c, j, g):
                k = NB * c + j
                act.wait_ge(g_mm, NG * k + g + 1)
                act.activation(g_sb[:, :, (j * NG + g) * GB:(j * NG + g + 1) * GB],
                               g_bank[g % 2][:, 0:GC].rearrange("p (i b) -> p i b", b=GB), ACT.Copy).then_inc(g_act, 1)

            def keep_z2(c):
                act.wait_ge(z2_mm, c + 1)
                act.activation(z2[:, :], misc_bank[:, 384:384 + CH], ACT.Copy).then_inc(z2_done, 1)

            def relu1(c):
                act.wait_ge(h1_mm, c + 1)
                for m in range(M1):
                    act.activation(h1[:, m, :], turn_bank[:, m * CH:(m + 1) * CH], ACT.Relu,
                                   bias=bt1[:, m:m + 1]).then_inc(h1_done, 1)

            def relu2(c):
                act.wait_ge(h2_mm, c + 1)
                for m in range(M2):
                    act.activation(h2[:, m, :], turn_bank[:, m * CH:(m + 1) * CH], ACT.Relu,
                                   bias=bt2[:, m:m + 1]).then_inc(h2_done, 1)

            def keep_y(c):
                act.wait_ge(y_mm, c + 1)
                act.activation(y_sb[:, bass.ds(c * CH, CH)], turn_bank[0:1, 0:CH], ACT.Copy).then_inc(mlp_through, 1)

            def later_blocks(c, has_previous):
                for j in range(1, NB):
                    keep_rep(c, j)
                    keep_x1(c, j - 1)
                    if j >= 2:
                        keep_g(c, j - 2, 0)
                        keep_g(c, j - 2, 2)
                    if has_previous:
                        (None, relu1, relu2, keep_y)[j](c - 1)

            act.sem_inc(mlp_through, 1)
            keep_turned(0)
            keep_rep(0, 0)
            later_blocks(0, False)
            act.wait_ge(mlp_in, 16 * 7)
            with act.Fori(1, NCH) as c:
                keep_turned(c)
                keep_x1(c - 1, 3)
                keep_g(c - 1, 2, 0)
                keep_g(c - 1, 2, 2)
                keep_rep(c, 0)
                keep_g(c - 1, 3, 0)
                keep_g(c - 1, 3, 2)
                keep_z2(c - 1)
                later_blocks(c, True)
            c = NCH - 1
            keep_x1(c, 3)
            keep_g(c, 2, 0)
            keep_g(c, 2, 2)
            keep_g(c, 3, 0)
            keep_g(c, 3, 2)
            keep_z2(c)
            relu1(c)
            relu2(c)
            keep_y(c)


def kernel(**inputs):
    import ml_dtypes
    import numpy as np
    import concourse.bacc as bacc
    from concourse.bass_utils import run_bass_kernel_spmd

    nc = bacc.Bacc("TRN2", target_bir_lowering=False, num_devices=1)
    arrays, args = {}, []

    def give(name, a):
        arrays[name] = np.ascontiguousarray(a)
        args.append(nc.dram_tensor(name, arrays[name].shape, mybir.dt.from_np(arrays[name].dtype),
                                   kind="ExternalInput").ap())
        return args.pop()

    x = {n: np.asarray(a) for n, a in inputs.items()}
    ids = give("ids", x["ids"].reshape(NCH, CH, M).transpose(1, 0, 2).reshape(CH, NCH * M))
    tables = [give(f"tbl_{f}", x[f"tbl_{f}"]) for f in range(M)]

    shifts = [s + 1 for s in range(19)] + [0]
    order = np.zeros((2, NT, P3), np.int64)
    select = np.zeros((3, M, NT + 1, P3), np.float32)
    fields = np.arange(M)
    for slot, shift in enumerate(shifts):
        t, r = divmod(slot, 3)
        other = (fields + shift) % M
        order[0, t, r * M:(r + 1) * M] = fields * M + other
        order[1, t, r * M:(r + 1) * M] = other * M + fields
        select[:, other, t, r * M + fields] = 0.5 if shift == 0 else 1.0
    for r in range(3):
        select[:, fields, NT, r * M + fields] = 1.0
    w0 = x["L0_rec_W0"][0]
    pair_w_a = give("pair_w_a", w0[order[0]].transpose(1, 0, 2))
    pair_w_b = give("pair_w_b", w0[order[1]].transpose(1, 0, 2))
    sel = give("select", select.reshape(P3, NT + 1, P3).astype(ml_dtypes.bfloat16))
    w1 = give("w1", x["L0_rec_W1"][0])
    w_top1 = give("w_top1", x["W_top1"][:2 * H])
    w_dense = give("w_dense", x["W_top1"][2 * H:])
    b_top1 = give("b_top1", x["b_top1"].reshape(M1, 128).T)
    w_top2 = give("w_top2", x["W_top2"])
    b_top2 = give("b_top2", x["b_top2"].reshape(M2, 128).T)
    w_top3 = give("w_top3", x["W_top3"].reshape(M2, 128).T)
    dense_t = give("dense_t", x["dense_ctx"].T)
    ident_b = give("ident_b", np.eye(128, dtype=ml_dtypes.bfloat16))
    own_row = give("own_row", np.repeat(np.eye(GB, dtype=np.float32), D, axis=0))
    y = nc.dram_tensor("y", (1, B), F32, kind="ExternalOutput").ap()
    build_tower(nc, ids, tables, pair_w_a, pair_w_b, sel, w1, w_top1, w_dense, b_top1, w_top2, b_top2, w_top3,
                dense_t, ident_b, own_row, y)
    result = run_bass_kernel_spmd(nc, [arrays], core_ids=[0])
    return np.asarray(result.results[0]["y"]).reshape(B, 1)
```

```python
from contextlib import ExitStack

import concourse.bass as bass
from concourse import mybir

F32 = mybir.dt.float32
BF16 = mybir.dt.bfloat16
F16 = mybir.dt.float16
I32 = mybir.dt.int32
ACT = mybir.ActivationFunctionType
ALU = mybir.AluOpType

B, M, D = 512, 39, 16
H = 128
CH = 128
NCH = B // CH
BB = 32
NB = CH // BB
GB = 8
NG = BB // GB
COLS = BB * D
P3 = 3 * M
NT = 7
ROWS = [P3] * 6 + [2 * M]
MO = M + 1
GC = MO * GB
DENSE, F1, F2 = 16, 512, 256
M1, M2 = F1 // 128, F2 // 128
SP = 125
VOCAB = [125000, 12500, 1250, 1000, 1250, 1000, 125000, 1250, 1250, 125000, 125000, 12500, 1250, 125000, 1000, 125000,
         1250, 1000, 1250, 1250, 1000, 1250, 1000, 125000, 125000, 1250, 1250, 125000, 1000, 125000, 1250, 1000, 1250,
         1000, 1250, 125000, 125000, 1250, 1250]
ORDER = [f for v in (1250, 1000) for f in range(M) if VOCAB[f] == v] + [f for f in range(M) if VOCAB[f] > 1250]
SETS = [(0, 8, 10), (8, 8, 10), (16, 9, 8)]
NS = 25


def build_tower(nc, ids, tables, pair_w_a, pair_w_b, select, w1, w_top1, w_dense, b_top1, w_top2, b_top2, w_top3,
                dense_t, ident_b, own_row, small_ids, row_ids, small_tables, y):
    with ExitStack() as ctx:
        def sb(name, shape, dt=F32):
            return ctx.enter_context(nc.sbuf_tensor(name, shape, dt))

        def bank(name):
            return ctx.enter_context(nc.psum_tensor(name, [128, 512], F32))

        def sem(name):
            return ctx.enter_context(nc.semaphore(name))

        ids_sb = sb("ids_sb", [128, NCH * M], I32)
        wa = sb("wa", [P3, NT, H])
        wb = sb("wb", [P3, NT, H])
        pair_w = sb("pair_w", [P3, NT, H])
        sel = sb("sel", [P3, NT + 1, P3], BF16)
        w1_sb = sb("w1_sb", [128, M, H])
        wt1 = sb("wt1", [128, 2, F1])
        wtd = sb("wtd", [DENSE, F1])
        bt1 = sb("bt1", [128, M1])
        wt2 = sb("wt2", [128, M1, F2])
        bt2 = sb("bt2", [128, M2])
        wt3 = sb("wt3", [128, M2])
        dense_sb = sb("dense_sb", [DENSE, B])
        idb = sb("idb", [128, 128], BF16)
        own = sb("own", [128, GB])
        emb = sb("emb", [128, NCH * M * D])
        rest = sb("rest", [128, M * D])
        parts = sb("parts", [128, 3, M, D], BF16)
        x3 = sb("x3", [P3, CH, D], BF16)
        xrep = sb("xrep", [P3, 2, COLS])
        prod = sb("prod", [128, 2, NT, COLS])
        x1 = sb("x1", [128, 2, NG * H])
        xblk = sb("xblk", [128, 2, NG, MO, GB])
        g_sb = sb("g_sb", [128, MO, CH])
        z2 = sb("z2", [128, CH])
        h1 = sb("h1", [128, M1, CH])
        h2 = sb("h2", [128, M2, CH])
        y_sb = sb("y_sb", [1, B])
        small_ids_i = sb("small_ids_i", [SP, NS * CH], I32)
        small_ids_h = sb("small_ids_h", [SP, NS * CH], F16)
        row_id = sb("row_id", [SP, len(SETS), 10])
        tab = [sb(f"tab{n}", [SP, w, rows, D]) for n, (_, w, rows) in enumerate(SETS)]
        tab_parts = [sb(f"tab_parts{n}", [SP, w, rows, 3, D], BF16) for n, (_, w, rows) in enumerate(SETS)]
        onehot = [buf[0:SP].bitcast(BF16)[:, 0:rows * w * CH].rearrange("p (r w b) -> p r w b", r=rows, w=w)
                  for buf, (_, w, rows) in zip((g_sb[:, :, :].rearrange("p i b -> p (i b)"),
                                                prod[:, :, :, :].rearrange("p a t n -> p (a t n)"),
                                                w1_sb[:, :, :].rearrange("p i h -> p (i h)")), SETS)]

        pair_bank = [bank("pair_bank0"), bank("pair_bank1")]
        turn_bank = bank("turn_bank")
        x1_bank = [bank("x1_bank0"), bank("x1_bank1")]
        g_bank = [bank("g_bank0"), bank("g_bank1")]
        misc_bank = bank("misc_bank")

        look_bank = [pair_bank[0], pair_bank[1], g_bank[0]]

        ids_in = sem("ids_in")
        pair_w_in = sem("pair_w_in")
        row_id_in = sem("row_id_in")
        small_ids_in = [sem(f"small_ids_in{n}") for n in range(len(SETS))]
        tab_in = [sem(f"tab_in{n}") for n in range(len(SETS))]
        small_ids_ok = sem("small_ids_ok")
        tab_hi = sem("tab_hi")
        tab_rest = sem("tab_rest")
        tab_mid = sem("tab_mid")
        tab_lo = sem("tab_lo")
        onehot_done = sem("onehot_done")
        looked_up = sem("looked_up")
        looked_ok = sem("looked_ok")
        small_in = sem("small_in")
        w1_in = sem("w1_in")
        mlp_in = sem("mlp_in")
        gathered = [sem(f"gathered{c}") for c in range(NCH)]
        chunk_in = sem("chunk_in")
        split_hi = sem("split_hi")
        split_left = sem("split_left")
        split_mid = sem("split_mid")
        split_done = sem("split_done")
        turned = sem("turned")
        x3_a = sem("x3_a")
        x3_b = sem("x3_b")
        rep_sel = sem("rep_sel")
        rep_done = sem("rep_done")
        pair_sel = sem("pair_sel")
        prod_done = sem("prod_done")
        pair_w_done = sem("pair_w_done")
        ones_done = sem("ones_done")
        xt_done = sem("xt_done")
        xblk_done = sem("xblk_done")
        x1_mm = sem("x1_mm")
        x1_done = sem("x1_done")
        g_mm = sem("g_mm")
        g_act = sem("g_act")
        g_dve = sem("g_dve")
        z2_mm = sem("z2_mm")
        z2_done = sem("z2_done")
        h1_mm = sem("h1_mm")
        h1_done = sem("h1_done")
        h2_mm = sem("h2_mm")
        h2_done = sem("h2_done")
        y_mm = sem("y_mm")
        mlp_through = sem("mlp_through")
        y_out = sem("y_out")

        def wait(eng, s, value):
            if not isinstance(value, int) or value > 0:
                eng.wait_ge(s, value)

        block = ctx.enter_context(nc.Block())

        @block.sync
        def _(sp):
            def land(c):
                sp.wait_ge(gathered[c], 16 * (M if c else M - NS))
                sp.sem_inc(chunk_in, 1)

            sp.dma_start(ids_sb[:, :], ids).then_inc(ids_in, 16)
            sp.dma_start(row_id[:, :, :], row_ids).then_inc(row_id_in, 16)
            for n, (f0, w, rows) in enumerate(SETS):
                of_set = slice(f0 * CH, (f0 + w) * CH)
                sp.dma_start(small_ids_i[:, of_set], small_ids[:, of_set].to_broadcast([SP, w * CH])).then_inc(small_ids_in[n], 16)
                sp.dma_start(tab[n][:, :, :, :], small_tables[n].rearrange("f (p r) d -> p f (r d)", p=SP)).then_inc(tab_in[n], 16)
            sp.dma_start(wa[:, :, :], pair_w_a).then_inc(pair_w_in, 16)
            sp.dma_start(wb[:, :, :], pair_w_b).then_inc(pair_w_in, 16)
            sp.dma_start(sel[:, :, :], select).then_inc(small_in, 16)
            sp.dma_start(idb[:, :], ident_b).then_inc(small_in, 16)
            sp.dma_start(own[:, :], own_row).then_inc(small_in, 16)
            land(0)
            sp.wait_ge(looked_up, len(SETS))
            sp.dma_start(w1_sb[:, :, :], w1.rearrange("(i j) h -> j i h", i=M)).then_inc(w1_in, 16)
            sp.dma_start(wt1[:, :, :], w_top1.rearrange("(k p) n -> p k n", p=128)).then_inc(mlp_in, 16)
            sp.dma_start(wtd[:, :], w_dense).then_inc(mlp_in, 16)
            sp.dma_start(bt1[:, :], b_top1).then_inc(mlp_in, 16)
            sp.dma_start(wt2[:, :, :], w_top2.rearrange("(k p) n -> p k n", p=128)).then_inc(mlp_in, 16)
            sp.dma_start(bt2[:, :], b_top2).then_inc(mlp_in, 16)
            sp.dma_start(wt3[:, :], w_top3).then_inc(mlp_in, 16)
            sp.dma_start(dense_sb[:, :], dense_t).then_inc(mlp_in, 16)
            for c in range(1, NCH):
                land(c)
            sp.wait_ge(mlp_through, NCH + 1)
            sp.dma_start(y, y_sb[:, :]).then_inc(y_out, 16)
            sp.wait_ge(y_out, 16)

        @block.gpsimd
        def _(pool):
            pool.wait_ge(ids_in, 16)
            for c in range(NCH):
                for f in range(0 if c else NS, M):
                    at = (c * M + f) * D
                    pool.indirect_dma_start(
                        out=emb[:, at:at + D], out_offset=None, in_=tables[f],
                        in_offset=bass.IndirectOffsetOnAxis(ap=ids_sb[:, c * M + f:c * M + f + 1], axis=0),
                    ).then_inc(gathered[c], 16)

        @block.tensor
        def _(pe):
            def turn(c):
                pe.wait_ge(split_done, c + 1)
                wait(pe, mlp_through, c)
                for half, to in ((0, turn_bank), (1, misc_bank)):
                    if half:
                        wait(pe, xblk_done, NB * c)
                    out = to[0:P3, :].bitcast(BF16).rearrange("p (d b) -> p d b", b=CH)
                    for d in range(D // 2):
                        mm = pe.transpose(out[:, d, :], parts[:, :, :, half * D // 2 + d].rearrange("b q i -> b (q i)"),
                                          idb[:, :])
                    mm.then_inc(turned, 1)

            def select_rep(c, j):
                k = NB * c + j
                wait(pe, prod_done, NT * k - 1)
                pe.matmul(pair_bank[0][0:P3, :], sel[:, NT, :], x3[:, j * BB:(j + 1) * BB, :],
                          start=True, stop=True).then_inc(rep_sel, 1)

            def select_pair(c, j, t):
                k = NB * c + j
                if t == 0:
                    wait(pe, prod_done, NT * k)
                elif t == 1:
                    pe.wait_ge(rep_done, k + 1)
                else:
                    wait(pe, prod_done, NT * k + t - 1)
                pe.matmul(pair_bank[(t + 1) % 2][0:ROWS[t], :], sel[:, t, 0:ROWS[t]], x3[:, j * BB:(j + 1) * BB, :],
                          start=True, stop=True).then_inc(pair_sel, 1)

            def turn_x(c, j):
                k = NB * c + j
                wait(pe, xblk_done, k)
                for g in range(NG):
                    col = (j * NG + g) * GB
                    mm = pe.matmul(misc_bank[:, g * MO:g * MO + M], x3[:, col:col + GB, :], sel[:, NT, 0:M],
                                   start=True, stop=True)
                mm.then_inc(xt_done, 1)

            def layer1(c, j, g, t0=0, t1=NT):
                k = NB * c + j
                if g == 0 and t0 == 0:
                    pe.wait_ge(prod_done, NT * (k + 1))
                    wait(pe, x1_done, k - 1)
                for t in range(t0, t1):
                    mm = pe.matmul(x1_bank[j % 2][:, g * H:(g + 1) * H], prod[0:ROWS[t], j % 2, t, g * 128:(g + 1) * 128],
                                   pair_w[0:ROWS[t], t, :], start=(t == 0), stop=(t == NT - 1))
                if g == NG - 1 and t1 == NT:
                    mm.then_inc(x1_mm, 1)

            def contract_d(c, j, g):
                k = NB * c + j
                if g == 0:
                    pe.wait_ge(x1_done, k + 1)
                    pe.wait_ge(xblk_done, k + 1)
                wait(pe, g_dve if g % 2 else g_act, 2 * k + g // 2)
                pe.matmul(g_bank[g % 2][:, 0:GC], x1[:, j % 2, g * H:(g + 1) * H],
                          xblk[:, j % 2, g, :, :].rearrange("p i b -> p (i b)"), start=True, stop=True).then_inc(g_mm, 1)

            def layer2(c, i0, i1):
                if i0 == 0:
                    pe.wait_ge(g_act, 2 * NB * (c + 1))
                    pe.wait_ge(g_dve, 2 * NB * (c + 1))
                    pe.wait_ge(mlp_through, c + 1)
                for i in range(i0, i1):
                    mm = pe.matmul(turn_bank[:, 0:CH], w1_sb[:, i, :], g_sb[:, i, :], start=(i == 0), stop=(i == M - 1))
                if i1 == M:
                    mm.then_inc(z2_mm, 1)

            def mlp1(c):
                pe.wait_ge(z2_done, c + 1)
                for m in range(M1):
                    out = turn_bank[:, m * CH:(m + 1) * CH]
                    cols = slice(m * 128, (m + 1) * 128)
                    pe.matmul(out, wt1[:, 0, cols], g_sb[:, M, :], start=True, stop=False)
                    pe.matmul(out, wt1[:, 1, cols], z2[:, :], start=False, stop=False)
                    mm = pe.matmul(out, wtd[:, cols], dense_sb[:, bass.ds(c * CH, CH)], start=False, stop=True)
                mm.then_inc(h1_mm, 1)

            def mlp2(c):
                pe.wait_ge(h1_done, M1 * (c + 1))
                for m in range(M2):
                    for k in range(M1):
                        mm = pe.matmul(turn_bank[:, m * CH:(m + 1) * CH], wt2[:, k, m * 128:(m + 1) * 128], h1[:, k, :],
                                       start=(k == 0), stop=(k == M1 - 1))
                mm.then_inc(h2_mm, 1)

            def mlp3(c):
                pe.wait_ge(h2_done, M2 * (c + 1))
                for k in range(M2):
                    mm = pe.matmul(turn_bank[0:1, 0:CH], wt3[:, k:k + 1], h2[:, k, :], start=(k == 0), stop=(k == M2 - 1))
                mm.then_inc(y_mm, 1)

            def later_blocks(c, has_previous):
                for j in range(1, NB):
                    select_rep(c, j)
                    select_pair(c, j, 0)
                    layer1(c, j - 1, 0)
                    if j == 1:
                        for t in range(1, NT):
                            select_pair(c, j, t)
                            half = (0, 4) if t % 2 else (4, NT)
                            layer1(c, j - 1, (t + 1) // 2, *half)
                    else:
                        for t in range(1, NT):
                            select_pair(c, j, t)
                            if t < NG:
                                layer1(c, j - 1, t)
                            else:
                                contract_d(c, j - 2, t - NG)
                        contract_d(c, j - 2, 3)
                    turn_x(c, j)
                    if has_previous:
                        (None, mlp1, mlp2, mlp3)[j](c - 1)

            for n, (f0, w, rows) in enumerate(SETS):
                pe.wait_ge(onehot_done, n + 1)
                pe.wait_ge(tab_hi, n + 1)
                pe.wait_ge(tab_mid, n + 1)
                pe.wait_ge(tab_lo, n + 1)
                for f in range(w):
                    for r in range(rows):
                        mm = pe.matmul(look_bank[n][:, f * 3 * D:(f + 1) * 3 * D], onehot[n][:, r, f, :],
                                       tab_parts[n][:, f, r, :, :], start=(r == 0), stop=(r == rows - 1))
                mm.then_inc(looked_up, 1)
            pe.wait_ge(small_in, 48)
            pe.wait_ge(looked_ok, len(SETS))
            turn(0)
            pe.wait_ge(x3_a, 1)
            pe.wait_ge(x3_b, 1)
            select_rep(0, 0)
            for t in range(NT):
                select_pair(0, 0, t)
            turn_x(0, 0)
            pe.wait_ge(pair_w_done, 1)
            pe.wait_ge(ones_done, 1)
            later_blocks(0, False)
            pe.wait_ge(w1_in, 16)
            pe.wait_ge(mlp_in, 16 * 7)

            def chunk(c):
                layer1(c - 1, 3, 0)
                layer1(c - 1, 3, 1)
                turn(c)
                layer1(c - 1, 3, 2)
                layer1(c - 1, 3, 3)
                contract_d(c - 1, 2, 0)
                contract_d(c - 1, 2, 1)
                contract_d(c - 1, 2, 2)
                contract_d(c - 1, 2, 3)
                pe.wait_ge(x3_a, c + 1)
                pe.wait_ge(x3_b, c + 1)
                select_rep(c, 0)
                select_pair(c, 0, 0)
                for g in range(NG):
                    contract_d(c - 1, 3, g)
                    if g < 2:
                        select_pair(c, 0, g + 1)
                for n in range(4):
                    select_pair(c, 0, n + 3)
                    layer2(c - 1, n * 10, min(n * 10 + 10, M))
                turn_x(c, 0)
                later_blocks(c, True)

            with pe.Fori(1, NCH - 1) as c:
                chunk(c)
            c = NCH - 1
            chunk(c)
            for g in range(NG):
                layer1(c, 3, g)
            for g in range(NG):
                contract_d(c, 2, g)
            for g in range(NG):
                contract_d(c, 3, g)
            layer2(c, 0, M)
            mlp1(c)
            mlp2(c)
            mlp3(c)

        @block.vector
        def _(dve):
            def split_rest(c, f0=0):
                n = (M - f0) * D
                dve.wait_ge(split_hi, c + 1)
                dve.tensor_tensor(rest[:, 0:n], emb[:, bass.ds(c * M * D + f0 * D, n)],
                                  parts[:, 0, f0:M, :].rearrange("b i d -> b (i d)"),
                                  ALU.subtract).then_inc(split_left, 1)

            def split_lo(c, f0=0):
                n = (M - f0) * D
                dve.wait_ge(split_mid, c + 1)
                dve.wait_ge(split_left, c + 1)
                dve.tensor_tensor(parts[:, 2, f0:M, :].rearrange("b i d -> b (i d)"), rest[:, 0:n],
                                  parts[:, 1, f0:M, :].rearrange("b i d -> b (i d)"),
                                  ALU.subtract).then_inc(split_done, 1)

            def one_hot(n):
                f0, w, rows = SETS[n]
                dve.wait_ge(small_ids_ok, n + 1)
                for r in range(rows):
                    last = dve.tensor_scalar(onehot[n][:, r, :, :].rearrange("p w b -> p (w b)"),
                                             small_ids_h[:, f0 * CH:(f0 + w) * CH], row_id[:, n, r:r + 1], None,
                                             ALU.is_equal)
                last.then_inc(onehot_done, 1)

            def table_rest(n):
                dve.wait_ge(tab_hi, n + 1)
                dve.tensor_tensor(tab[n][:, :, :, :], tab[n][:, :, :, :], tab_parts[n][:, :, :, 0, :],
                                  ALU.subtract).then_inc(tab_rest, 1)

            def table_lo(n):
                dve.wait_ge(tab_mid, n + 1)
                dve.tensor_tensor(tab_parts[n][:, :, :, 2, :], tab[n][:, :, :, :], tab_parts[n][:, :, :, 1, :],
                                  ALU.subtract).then_inc(tab_lo, 1)

            def keep_turned(c):
                dve.wait_ge(turned, 2 * c + 1)
                dve.tensor_copy(x3[:, :, 0:D // 2].rearrange("p b d -> p d b"),
                                turn_bank[0:P3, :].bitcast(BF16).rearrange("p (d b) -> p d b", b=CH)).then_inc(x3_a, 1)

            def multiply(c, j, t):
                k = NB * c + j
                if t == 0:
                    dve.wait_ge(rep_done, k + 1)
                    wait(dve, x1_mm, k - 1)
                dve.wait_ge(pair_sel, NT * k + t + 1)
                dve.tensor_tensor(prod[0:ROWS[t], j % 2, t, :], pair_bank[(t + 1) % 2][0:ROWS[t], :],
                                  xrep[0:ROWS[t], j % 2, :], ALU.mult).then_inc(prod_done, 1)

            def spread(c, j):
                k = NB * c + j
                dve.wait_ge(xt_done, k + 1)
                wait(dve, g_mm, NG * (k - 1))
                dve.tensor_tensor(
                    xblk[:, j % 2, :, 0:M, :],
                    misc_bank[:, 0:NG * MO].rearrange("p (g i) -> p g i", g=NG)[:, :, 0:M].unsqueeze(3).to_broadcast([128, NG, M, GB]),
                    own[:, :].unsqueeze(1).unsqueeze(1).to_broadcast([128, NG, M, GB]),
                    ALU.mult).then_inc(xblk_done, 1)

            def keep_g(c, j, g):
                k = NB * c + j
                dve.wait_ge(g_mm, NG * k + g + 1)
                dve.tensor_copy(g_sb[:, :, (j * NG + g) * GB:(j * NG + g + 1) * GB],
                                g_bank[g % 2][:, 0:GC].rearrange("p (i b) -> p i b", b=GB)).then_inc(g_dve, 1)

            def later_blocks(c, split_at, has_next=True):
                for j in range(1, NB):
                    multiply(c, j, 0)
                    multiply(c, j, 1)
                    for t in range(2, NT - 1):
                        multiply(c, j, t)
                    if j >= 2:
                        keep_g(c, j - 2, 1)
                    multiply(c, j, NT - 1)
                    if j >= 2:
                        keep_g(c, j - 2, 3)
                    if j == split_at and has_next:
                        split_rest(c + 1)
                    spread(c, j)
                    if j == split_at and has_next:
                        split_lo(c + 1)

            dve.wait_ge(row_id_in, 16)
            one_hot(0)
            table_rest(0)
            one_hot(1)
            table_lo(0)
            table_rest(1)
            one_hot(2)
            table_lo(1)
            table_rest(2)
            table_lo(2)
            split_rest(0, NS)
            dve.wait_ge(pair_w_in, 32)
            dve.tensor_tensor(pair_w[:, :, :], wa[:, :, :], wb[:, :, :], ALU.add).then_inc(pair_w_done, 1)
            split_lo(0, NS)
            dve.wait_ge(small_in, 48)
            dve.tensor_copy(xblk[:, :, :, M, :].rearrange("p a g b -> p (a g) b"),
                            own[:, :].unsqueeze(1).to_broadcast([128, 2 * NG, GB])).then_inc(ones_done, 1)
            keep_turned(0)
            for t in range(NT):
                multiply(0, 0, t)
            spread(0, 0)
            later_blocks(0, 3)

            def chunk(c, has_next):
                keep_turned(c)
                keep_g(c - 1, 2, 1)
                keep_g(c - 1, 2, 3)
                multiply(c, 0, 0)
                multiply(c, 0, 1)
                keep_g(c - 1, 3, 1)
                multiply(c, 0, 2)
                keep_g(c - 1, 3, 3)
                for t in range(3, NT):
                    multiply(c, 0, t)
                spread(c, 0)
                later_blocks(c, 2, has_next)

            with dve.Fori(1, NCH - 1) as c:
                chunk(c, True)
            c = NCH - 1
            chunk(c, False)
            keep_g(c, 2, 1)
            keep_g(c, 2, 3)
            keep_g(c, 3, 1)
            keep_g(c, 3, 3)

        @block.scalar
        def _(act):
            def keep_turned(c):
                act.wait_ge(turned, 2 * c + 2)
                act.activation(x3[:, :, D // 2:D].rearrange("p b d -> p d b"),
                               misc_bank[0:P3, :].bitcast(BF16).rearrange("p (d b) -> p d b", b=CH),
                               ACT.Copy).then_inc(x3_b, 1)

            def split_first(c, f0=0):
                act.wait_ge(chunk_in, c + 1)
                act.activation(parts[:, 0, f0:M, :].rearrange("b i d -> b (i d)"),
                               emb[:, bass.ds(c * M * D + f0 * D, (M - f0) * D)], ACT.Copy).then_inc(split_hi, 1)

            def split_second(c, f0=0):
                act.wait_ge(split_left, c + 1)
                act.activation(parts[:, 1, f0:M, :].rearrange("b i d -> b (i d)"), rest[:, 0:(M - f0) * D],
                               ACT.Copy).then_inc(split_mid, 1)

            def keep_rep(c, j):
                k = NB * c + j
                act.wait_ge(rep_sel, k + 1)
                wait(act, prod_done, NT * (k - 1))
                act.activation(xrep[:, j % 2, :], pair_bank[0][0:P3, :], ACT.Copy).then_inc(rep_done, 1)

            def keep_x1(c, j):
                k = NB * c + j
                act.wait_ge(x1_mm, k + 1)
                wait(act, g_mm, NG * (k - 1))
                act.activation(x1[:, j % 2, :], x1_bank[j % 2][:, :], ACT.Copy).then_inc(x1_done, 1)

            def keep_g(c, j, g):
                k = NB * c + j
                act.wait_ge(g_mm, NG * k + g + 1)
                act.activation(g_sb[:, :, (j * NG + g) * GB:(j * NG + g + 1) * GB],
                               g_bank[g % 2][:, 0:GC].rearrange("p (i b) -> p i b", b=GB), ACT.Copy).then_inc(g_act, 1)

            def keep_z2(c):
                act.wait_ge(z2_mm, c + 1)
                act.activation(z2[:, :], turn_bank[:, 0:CH], ACT.Copy).then_inc(z2_done, 1)

            def relu1(c):
                act.wait_ge(h1_mm, c + 1)
                for m in range(M1):
                    act.activation(h1[:, m, :], turn_bank[:, m * CH:(m + 1) * CH], ACT.Relu,
                                   bias=bt1[:, m:m + 1]).then_inc(h1_done, 1)

            def relu2(c):
                act.wait_ge(h2_mm, c + 1)
                for m in range(M2):
                    act.activation(h2[:, m, :], turn_bank[:, m * CH:(m + 1) * CH], ACT.Relu,
                                   bias=bt2[:, m:m + 1]).then_inc(h2_done, 1)

            def keep_y(c):
                act.wait_ge(y_mm, c + 1)
                act.activation(y_sb[:, bass.ds(c * CH, CH)], turn_bank[0:1, 0:CH], ACT.Copy).then_inc(mlp_through, 1)

            def later_blocks(c, split_at, has_previous, has_next=True):
                for j in range(1, NB):
                    keep_rep(c, j)
                    keep_x1(c, j - 1)
                    if j >= 2:
                        keep_g(c, j - 2, 0)
                    if j == split_at and has_next:
                        split_first(c + 1)
                    if j >= 2:
                        keep_g(c, j - 2, 2)
                    if j == split_at and has_next:
                        split_second(c + 1)
                    if has_previous:
                        (None, relu1, relu2, keep_y)[j](c - 1)

            act.sem_inc(mlp_through, 1)
            for n, (f0, w, rows) in enumerate(SETS):
                act.wait_ge(small_ids_in[n], 16)
                act.activation(small_ids_h[:, f0 * CH:(f0 + w) * CH], small_ids_i[:, f0 * CH:(f0 + w) * CH],
                               ACT.Copy).then_inc(small_ids_ok, 1)
                act.wait_ge(tab_in[n], 16)
                act.activation(tab_parts[n][:, :, :, 0, :], tab[n][:, :, :, :], ACT.Copy).then_inc(tab_hi, 1)
                if n:
                    act.wait_ge(tab_rest, n)
                    act.activation(tab_parts[n - 1][:, :, :, 1, :], tab[n - 1][:, :, :, :], ACT.Copy).then_inc(tab_mid, 1)
            n = len(SETS) - 1
            act.wait_ge(tab_rest, n + 1)
            act.activation(tab_parts[n][:, :, :, 1, :], tab[n][:, :, :, :], ACT.Copy).then_inc(tab_mid, 1)
            split_first(0, NS)
            split_second(0, NS)
            for n, (f0, w, rows) in enumerate(SETS):
                act.wait_ge(looked_up, n + 1)
                act.activation(parts[:, :, f0:f0 + w, :],
                               look_bank[n][:, 0:w * 3 * D].rearrange("b (f q d) -> b q f d", q=3, d=D),
                               ACT.Copy).then_inc(looked_ok, 1)
            keep_turned(0)
            keep_rep(0, 0)
            later_blocks(0, 3, False)
            act.wait_ge(mlp_in, 16 * 7)

            def chunk(c, has_next):
                keep_turned(c)
                keep_x1(c - 1, 3)
                keep_g(c - 1, 2, 0)
                keep_g(c - 1, 2, 2)
                keep_rep(c, 0)
                keep_g(c - 1, 3, 0)
                keep_g(c - 1, 3, 2)
                keep_z2(c - 1)
                later_blocks(c, 2, True, has_next)

            with act.Fori(1, NCH - 1) as c:
                chunk(c, True)
            c = NCH - 1
            chunk(c, False)
            keep_x1(c, 3)
            keep_g(c, 2, 0)
            keep_g(c, 2, 2)
            keep_g(c, 3, 0)
            keep_g(c, 3, 2)
            keep_z2(c)
            relu1(c)
            relu2(c)
            keep_y(c)


def kernel(**inputs):
    import ml_dtypes
    import numpy as np
    import concourse.bacc as bacc
    from concourse.bass_utils import run_bass_kernel_spmd

    nc = bacc.Bacc("TRN2", target_bir_lowering=False, num_devices=1)
    arrays, args = {}, []

    def give(name, a):
        arrays[name] = np.ascontiguousarray(a)
        args.append(nc.dram_tensor(name, arrays[name].shape, mybir.dt.from_np(arrays[name].dtype),
                                   kind="ExternalInput").ap())
        return args.pop()

    x = {n: np.asarray(a) for n, a in inputs.items()}
    by_field = x["ids"][:, ORDER]
    ids = give("ids", by_field.reshape(NCH, CH, M).transpose(1, 0, 2).reshape(CH, NCH * M))
    tables = [give(f"tbl_{f}", x[f"tbl_{f}"]) for f in ORDER]
    small_tables = [give(f"small_{n}", np.stack([x[f"tbl_{f}"] for f in ORDER[f0:f0 + w]]))
                    for n, (f0, w, _) in enumerate(SETS)]
    small_ids = give("small_ids", by_field[:CH, :NS].T.reshape(1, NS * CH))
    row_ids = np.zeros((SP, len(SETS), 10), np.float32)
    for n, (_, _, rows) in enumerate(SETS):
        row_ids[:, n, :rows] = np.arange(SP * rows).reshape(SP, rows)
    row_ids = give("row_ids", row_ids)

    shifts = [s + 1 for s in range(19)] + [0]
    order = np.zeros((2, NT, P3), np.int64)
    select = np.zeros((3, M, NT + 1, P3), np.float32)
    fields = np.arange(M)
    at = np.array(ORDER)
    for slot, shift in enumerate(shifts):
        t, r = divmod(slot, 3)
        other = (fields + shift) % M
        order[0, t, r * M:(r + 1) * M] = at[fields] * M + at[other]
        order[1, t, r * M:(r + 1) * M] = at[other] * M + at[fields]
        select[:, other, t, r * M + fields] = 0.5 if shift == 0 else 1.0
    for r in range(3):
        select[:, fields, NT, r * M + fields] = 1.0
    w0 = x["L0_rec_W0"][0]
    pair_w_a = give("pair_w_a", w0[order[0]].transpose(1, 0, 2))
    pair_w_b = give("pair_w_b", w0[order[1]].transpose(1, 0, 2))
    sel = give("select", select.reshape(P3, NT + 1, P3).astype(ml_dtypes.bfloat16))
    w1 = give("w1", x["L0_rec_W1"][0].reshape(M, H, H)[ORDER].reshape(M * H, H))
    w_top1 = give("w_top1", x["W_top1"][:2 * H])
    w_dense = give("w_dense", x["W_top1"][2 * H:])
    b_top1 = give("b_top1", x["b_top1"].reshape(M1, 128).T)
    w_top2 = give("w_top2", x["W_top2"])
    b_top2 = give("b_top2", x["b_top2"].reshape(M2, 128).T)
    w_top3 = give("w_top3", x["W_top3"].reshape(M2, 128).T)
    dense_t = give("dense_t", x["dense_ctx"].T)
    ident_b = give("ident_b", np.eye(128, dtype=ml_dtypes.bfloat16))
    own_row = give("own_row", np.repeat(np.eye(GB, dtype=np.float32), D, axis=0))
    y = nc.dram_tensor("y", (1, B), F32, kind="ExternalOutput").ap()
    build_tower(nc, ids, tables, pair_w_a, pair_w_b, sel, w1, w_top1, w_dense, b_top1, w_top2, b_top2, w_top3,
                dense_t, ident_b, own_row, small_ids, row_ids, small_tables, y)
    result = run_bass_kernel_spmd(nc, [arrays], core_ids=[0])
    return np.asarray(result.results[0]["y"]).reshape(B, 1)
```

```python
from contextlib import ExitStack

import concourse.bass as bass
from concourse import mybir

F32 = mybir.dt.float32
BF16 = mybir.dt.bfloat16
F16 = mybir.dt.float16
F32R = mybir.dt.float32r
I32 = mybir.dt.int32
ACT = mybir.ActivationFunctionType
ALU = mybir.AluOpType

B, M, D = 512, 39, 16
H = 128
CH = 128
NCH = B // CH
BB = 32
NB = CH // BB
GB = 8
NG = BB // GB
COLS = BB * D
P3 = 3 * M
PAIRS = M * (M + 1) // 2
NT = -(-PAIRS // 128)
FULL = NT - 1
LEFT = PAIRS - 128 * FULL
ROWS = [128] * FULL + [96]
DVE_ROUNDS = (1, 3, 5)
ACT_TO = [n - sum(m < n for m in DVE_ROUNDS) for n in range(NT + 1)]
DVE_TO = [n - ACT_TO[n] for n in range(NT + 1)]
DVE_X1_AT = 2
LAG = 2
MO = M + 1
GC = MO * GB
SPREAD = 16 * (GB // 2)
DENSE, F1, F2 = 16, 512, 256
M1, M2 = F1 // 128, F2 // 128
SP = 125
VOCAB = [125000, 12500, 1250, 1000, 1250, 1000, 125000, 1250, 1250, 125000, 125000, 12500, 1250, 125000, 1000, 125000,
         1250, 1000, 1250, 1250, 1000, 1250, 1000, 125000, 125000, 1250, 1250, 125000, 1000, 125000, 1250, 1000, 1250,
         1000, 1250, 125000, 125000, 1250, 1250]
ORDER = [f for v in (1250, 1000) for f in range(M) if VOCAB[f] == v] + [f for f in range(M) if VOCAB[f] > 1250]
SETS = [(0, 8, 10), (8, 8, 10), (16, 9, 8)]
NS = 25


def build_tower(nc, ids, tables, pair_w_a, pair_w_b, touches, select, w1, w_top1, w_dense, b_top1, w_top2, b_top2, w_top3,
                dense_t, ident_b, ident_f, parity_row, small_ids, row_ids, small_tables, y):
    with ExitStack() as ctx:
        def sb(name, shape, dt=F32):
            return ctx.enter_context(nc.sbuf_tensor(name, shape, dt))

        def bank(name):
            return ctx.enter_context(nc.psum_tensor(name, [128, 512], F32))

        def sem(name):
            return ctx.enter_context(nc.semaphore(name))

        ids_sb = sb("ids_sb", [128, NCH * M], I32)
        wa = sb("wa", [128, NT, H])
        wb = sb("wb", [128, NT, H])
        pair_w = sb("pair_w", [128, NT, H])
        pair_w_hi = sb("pair_w_hi", [128, NT, H], F32R)
        pair_w_lo = sb("pair_w_lo", [128, FULL, H], F32R)
        touch = sb("touch", [128, NT, M])
        sel = sb("sel", [P3, NT, 128], BF16)
        wt1 = sb("wt1", [128, 2, F1])
        wtd = sb("wtd", [DENSE, F1])
        bt1 = sb("bt1", [128, M1])
        wt2 = sb("wt2", [128, M1, F2])
        bt2 = sb("bt2", [128, M2])
        wt3 = sb("wt3", [128, M2])
        dense_sb = sb("dense_sb", [DENSE, B])
        idb = sb("idb", [128, 128], BF16)
        idf = sb("idf", [128, 128])
        parity = sb("parity", [128, 2])
        emb = sb("emb", [128, NCH * M * D])
        rest = sb("rest", [128, M * D])
        parts = sb("parts", [128, 3, M, D], BF16)
        x3 = sb("x3", [P3, CH, D], BF16)
        x1h = sb("x1h", [H, COLS])
        x1_hi = sb("x1_hi", [128, 2, NG * H], F32R)
        x1_lo = sb("x1_lo", [128, 2, NG * H], F32R)
        xs = sb("xs", [128, 2, NG, 2, MO], F32R)
        xblk = sb("xblk", [128, 2, 2, NG, GB, MO], F32R)
        z2 = sb("z2", [128, CH])
        h1 = sb("h1", [128, M1, CH])
        h2 = sb("h2", [128, M2, CH])
        y_sb = sb("y_sb", [1, B])

        with ExitStack() as early:
            def sb_early(name, shape, dt=F32):
                return early.enter_context(nc.sbuf_tensor(name, shape, dt))

            small_ids_i = sb_early("small_ids_i", [SP, NS * CH], I32)
            small_ids_h = sb_early("small_ids_h", [SP, NS * CH], F16)
            row_id = sb_early("row_id", [SP, len(SETS), 10])
            tab = [sb_early(f"tab{n}", [SP, w, rows, D]) for n, (_, w, rows) in enumerate(SETS)]
            tab_parts = [sb_early(f"tab_parts{n}", [SP, w, rows, 3, D], BF16) for n, (_, w, rows) in enumerate(SETS)]
            onehot = [sb_early(f"onehot{n}", [SP, rows, w, CH], BF16) for n, (_, w, rows) in enumerate(SETS)]

        prod = sb("prod", [128, NT, COLS])
        prod_hi = sb("prod_hi", [128, 2, NT, COLS], F32R)
        prod_lo = sb("prod_lo", [128, 2, FULL, COLS], F32R)
        g_sb = sb("g_sb", [128, MO, CH])
        w1_sb = sb("w1_sb", [128, M, H])

        pair_bank = [bank("pair_bank0"), bank("pair_bank1")]
        turn_bank = bank("turn_bank")
        x1_bank = bank("x1_bank")
        x1_turn_bank = bank("x1_turn_bank")
        g_bank = [bank("g_bank0"), bank("g_bank1")]
        misc_bank = bank("misc_bank")
        h1_banks = ([turn_bank] * M1, [pair_bank[0], pair_bank[1], x1_bank, misc_bank])
        h2_banks = ([turn_bank] * M2, [turn_bank, g_bank[0]])
        y_bank = (turn_bank, g_bank[1])
        look_bank = [pair_bank[0], pair_bank[1], g_bank[0]]

        ids_in = sem("ids_in")
        pair_w_in = sem("pair_w_in")
        row_id_in = sem("row_id_in")
        small_ids_in = [sem(f"small_ids_in{n}") for n in range(len(SETS))]
        tab_in = [sem(f"tab_in{n}") for n in range(len(SETS))]
        small_ids_ok = sem("small_ids_ok")
        tab_hi = sem("tab_hi")
        tab_rest = sem("tab_rest")
        tab_mid = sem("tab_mid")
        tab_lo = sem("tab_lo")
        onehot_done = sem("onehot_done")
        looked_up = sem("looked_up")
        looked_ok = sem("looked_ok")
        small_in = sem("small_in")
        w1_in = sem("w1_in")
        mlp_in = sem("mlp_in")
        gathered = [sem(f"gathered{c}") for c in range(NCH)]
        chunk_in = sem("chunk_in")
        split_left = sem("split_left")
        split_mid = sem("split_mid")
        split_done = sem("split_done")
        turned = sem("turned")
        x3_a = sem("x3_a")
        x3_b = sem("x3_b")
        pair_sel = sem("pair_sel")
        sq_done = sem("sq_done")
        hi_act = sem("hi_act")
        hi_dve = sem("hi_dve")
        lo_done = sem("lo_done")
        pair_w_sum = sem("pair_w_sum")
        touched = sem("touched")
        pair_w_done = sem("pair_w_done")
        pair_w_split = sem("pair_w_split")
        xs_ones = sem("xs_ones")
        xt_done = sem("xt_done")
        xs_hi_done = sem("xs_hi_done")
        xs_lo_done = sem("xs_lo_done")
        xblk_zero = sem("xblk_zero")
        xblk_done = sem("xblk_done")
        x1_mm = sem("x1_mm")
        x1_kept = sem("x1_kept")
        x1_turned = sem("x1_turned")
        x1_rounded = sem("x1_rounded")
        x1_done = sem("x1_done")
        g_mm = sem("g_mm")
        g_act = sem("g_act")
        g_dve = sem("g_dve")
        z2_mm = sem("z2_mm")
        z2_done = sem("z2_done")
        h1_mm = sem("h1_mm")
        h1_done = sem("h1_done")
        h2_mm = sem("h2_mm")
        h2_done = sem("h2_done")
        y_mm = sem("y_mm")
        mlp_through = sem("mlp_through")
        y_out = sem("y_out")

        def wait(eng, s, value):
            if not isinstance(value, int) or value > 0:
                eng.wait_ge(s, value)

        def upper(ap):
            return ap.bitcast(BF16).rearrange("p (n two) -> p n two", two=2)[:, :, 1]

        def flat(ap):
            return ap.rearrange("p f r d -> p (f r d)")

        block = ctx.enter_context(nc.Block())

        @block.sync
        def _(sp):
            def spread(c, j):
                k = NB * c + j
                sp.wait_ge(xs_lo_done, k + 1)
                for b in range(0, GB, 2):
                    rows = slice(b * D, (b + 2) * D)
                    sp.dma_start(xblk[rows, j % 2, :, :, b:b + 2, :].rearrange("p q g e i -> p (q g) (e i)").bitcast(F32),
                                 xs[rows, :, :, :, :].rearrange("p q g e i -> p (q g) (e i)").bitcast(F32)
                                 ).then_inc(xblk_done, 16)

            sp.dma_start(ids_sb[:, :], ids).then_inc(ids_in, 16)
            sp.dma_start(row_id[:, :, :], row_ids).then_inc(row_id_in, 16)
            for n, (f0, w, rows) in enumerate(SETS):
                of_set = slice(f0 * CH, (f0 + w) * CH)
                sp.dma_start(small_ids_i[:, of_set], small_ids[:, of_set].to_broadcast([SP, w * CH])).then_inc(small_ids_in[n], 16)
                sp.dma_start(tab[n][:, :, :, :], small_tables[n].rearrange("f (p r) d -> p f (r d)", p=SP)).then_inc(tab_in[n], 16)
            sp.dma_start(wa[:, :, :], pair_w_a).then_inc(pair_w_in, 16)
            sp.dma_start(wb[:, :, :], pair_w_b).then_inc(pair_w_in, 16)
            sp.dma_start(touch[:, :, :], touches).then_inc(pair_w_in, 16)
            sp.dma_start(sel[:, :, :], select).then_inc(small_in, 16)
            sp.dma_start(idb[:, :], ident_b).then_inc(small_in, 16)
            sp.dma_start(idf[:, :], ident_f).then_inc(small_in, 16)
            sp.dma_start(parity[:, :], parity_row).then_inc(small_in, 16)
            sp.wait_ge(looked_up, len(SETS))
            sp.dma_start(w1_sb[:, :, :], w1.rearrange("(i j) h -> j i h", i=M)).then_inc(w1_in, 16)
            sp.dma_start(wt1[:, :, :], w_top1.rearrange("(k p) n -> p k n", p=128)).then_inc(mlp_in, 16)
            sp.dma_start(wtd[:, :], w_dense).then_inc(mlp_in, 16)
            sp.dma_start(bt1[:, :], b_top1).then_inc(mlp_in, 16)
            sp.dma_start(wt2[:, :, :], w_top2.rearrange("(k p) n -> p k n", p=128)).then_inc(mlp_in, 16)
            sp.dma_start(bt2[:, :], b_top2).then_inc(mlp_in, 16)
            sp.dma_start(wt3[:, :], w_top3).then_inc(mlp_in, 16)
            sp.dma_start(dense_sb[:, :], dense_t).then_inc(mlp_in, 16)
            sp.wait_ge(xblk_zero, 2)
            sp.wait_ge(xs_ones, 1)
            with sp.Fori(0, NCH) as c:
                for j in range(NB):
                    spread(c, j)
            sp.wait_ge(mlp_through, NCH + 1)
            sp.dma_start(y, y_sb[:, :]).then_inc(y_out, 16)
            sp.wait_ge(y_out, 16)

        @block.gpsimd
        def _(pool):
            def land(c):
                pool.wait_ge(gathered[c], 16 * (M if c else M - NS))
                pool.sem_inc(chunk_in, 1)

            pool.wait_ge(ids_in, 16)
            for c in range(NCH):
                for f in range(0 if c else NS, M):
                    at = (c * M + f) * D
                    pool.indirect_dma_start(
                        out=emb[:, at:at + D], out_offset=None, in_=tables[f],
                        in_offset=bass.IndirectOffsetOnAxis(ap=ids_sb[:, c * M + f:c * M + f + 1], axis=0),
                    ).then_inc(gathered[c], 16)
                    if c and f == 2:
                        land(c - 1)
            land(NCH - 1)

        @block.tensor
        def _(pe):
            def turn(c):
                pe.wait_ge(split_mid, c + 1)
                pe.wait_ge(split_done, c + 1)
                wait(pe, mlp_through, c)
                for half, to in ((0, turn_bank), (1, misc_bank)):
                    if half:
                        wait(pe, xs_lo_done, NB * c)
                    out = to[0:P3, :].bitcast(BF16).rearrange("p (d b) -> p d b", b=CH)
                    for d in range(D // 2):
                        mm = pe.transpose(out[:, d, :], parts[:, :, :, half * D // 2 + d].rearrange("b q i -> b (q i)"),
                                          idb[:, :])
                    mm.then_inc(turned, 1)

            def select_pair(c, j, t):
                n = NT * (NB * c + j) + t
                wait(pe, sq_done, n - 1)
                pe.matmul(pair_bank[(j * NT + t) % 2][0:ROWS[t], :], sel[:, t, 0:ROWS[t]], x3[:, j * BB:(j + 1) * BB, :],
                          start=True, stop=True).then_inc(pair_sel, 1)

            def turn_x(c, j):
                k = NB * c + j
                wait(pe, xs_lo_done, k)
                for g in range(NG):
                    col = (j * NG + g) * GB
                    mm = pe.matmul(misc_bank[:, g * MO:g * MO + M], x3[:, col:col + GB, :], sel[:, 0, 0:M],
                                   start=True, stop=True)
                mm.then_inc(xt_done, 1)

            def layer1(c, j, n):
                k = NB * c + j
                t = n
                pe.wait_ge(lo_done, NT * k + n + 1)
                if n == 0:
                    wait(pe, x1_kept, k)
                p = slice(0, ROWS[t])
                mm = pe.matmul(x1_bank[:, :], pair_w_hi[p, t, :], prod_hi[p, j % 2, t, :], start=(n == 0), stop=(n == FULL))
                if n < FULL:
                    pe.matmul(x1_bank[:, :], pair_w_hi[p, t, :], prod_lo[p, j % 2, t, :], start=False, stop=False)
                    pe.matmul(x1_bank[:, :], pair_w_lo[p, t, :], prod_hi[p, j % 2, t, :], start=False, stop=False)
                if n == NT - 1:
                    mm.then_inc(x1_mm, 1)

            def turn_x1(c, j):
                k = NB * c + j
                pe.wait_ge(x1_kept, k + 1)
                wait(pe, x1_done, 2 * k)
                for g in range(NG):
                    mm = pe.transpose(x1_turn_bank[:, g * H:(g + 1) * H], x1h[:, g * 128:(g + 1) * 128], idf[:, :])
                mm.then_inc(x1_turned, 1)

            def contract_d(c, j, g):
                k = NB * c + j
                if g == 0:
                    pe.wait_ge(x1_rounded, k + 1)
                    pe.wait_ge(xblk_done, SPREAD * (k + 1))
                wait(pe, g_dve if g % 2 else g_act, 2 * k + g // 2)
                out = g_bank[g % 2][:, 0:GC]
                units = slice(g * H, (g + 1) * H)
                b_hi, b_lo = (xblk[:, j % 2, q, g, :, :].rearrange("p b i -> p (b i)") for q in range(2))
                pe.matmul(out, x1_hi[:, j % 2, units], b_hi, start=True, stop=False)
                pe.matmul(out, x1_hi[:, j % 2, units], b_lo, start=False, stop=False)
                if g % (NG // 2) == 0:
                    pe.wait_ge(x1_done, 2 * k + g // (NG // 2) + 1)
                pe.matmul(out, x1_lo[:, j % 2, units], b_hi, start=False, stop=True).then_inc(g_mm, 1)

            def layer2(c, i0, i1):
                if i0 == 0:
                    pe.wait_ge(g_act, 2 * NB * (c + 1))
                    pe.wait_ge(g_dve, 2 * NB * (c + 1))
                    pe.wait_ge(mlp_through, c + 1)
                for i in range(i0, i1):
                    mm = pe.matmul(turn_bank[:, 0:CH], w1_sb[:, i, :], g_sb[:, i, :], start=(i == 0), stop=(i == M - 1))
                if i1 == M:
                    mm.then_inc(z2_mm, 1)

            def columns(banks, m):
                return banks[m][:, m * CH:(m + 1) * CH]

            def h1_part(c, m, part, last=False):
                cols = slice(m * 128, (m + 1) * 128)
                w, rows = ((wtd[:, cols], dense_sb[:, bass.ds(c * CH, CH)]), (wt1[:, 0, cols], g_sb[:, M, :]),
                           (wt1[:, 1, cols], z2[:, :]))[part]
                return pe.matmul(columns(h1_banks[last], m), w, rows, start=(part == 0), stop=(part == 2))

            def mlp1(c):
                pe.wait_ge(z2_done, c + 1)
                for m in range(M1):
                    for part in range(3):
                        mm = h1_part(c, m, part)
                    mm.then_inc(h1_mm, 1)

            def last_mlp1_dense():
                pe.wait_ge(xs_lo_done, NB * NCH)
                for m in range(M1):
                    h1_part(NCH - 1, m, 0, True)

            def last_mlp1():
                for m in range(M1):
                    h1_part(NCH - 1, m, 1, True)
                pe.wait_ge(z2_done, NCH)
                for m in range(M1):
                    h1_part(NCH - 1, m, 2, True).then_inc(h1_mm, 1)

            def mlp2(c, last=False):
                if not last:
                    pe.wait_ge(h1_done, M1 * (c + 1))
                for m in range(M2):
                    for k in range(M1):
                        if last and m == 0:
                            pe.wait_ge(h1_done, M1 * c + k + 1)
                        mm = pe.matmul(columns(h2_banks[last], m), wt2[:, k, m * 128:(m + 1) * 128], h1[:, k, :],
                                       start=(k == 0), stop=(k == M1 - 1))
                    mm.then_inc(h2_mm, 1)

            def mlp3(c, last=False):
                if not last:
                    pe.wait_ge(h2_done, M2 * (c + 1))
                for k in range(M2):
                    if last:
                        pe.wait_ge(h2_done, M2 * c + k + 1)
                    mm = pe.matmul(y_bank[last][0:1, 0:CH], wt3[:, k:k + 1], h2[:, k, :], start=(k == 0),
                                   stop=(k == M2 - 1))
                mm.then_inc(y_mm, 1)

            def later_blocks(c, has_previous):
                for j in range(1, NB):
                    for n in range(NT):
                        select_pair(c, j, n)
                        layer1(c, j - 1, n)
                        if j >= 2 and n == 0:
                            turn_x1(c, j - 2)
                        if j >= 2 and n >= NT - NG:
                            contract_d(c, j - 2, n - (NT - NG))
                    turn_x(c, j)
                    if has_previous:
                        (None, mlp1, mlp2, mlp3)[j](c - 1)

            for n, (f0, w, rows) in enumerate(SETS):
                if n == len(SETS) - 1:
                    pe.wait_ge(pair_w_in, 48)
                    for w_pair in (wa, wb):
                        for t in range(NT):
                            mm = pe.matmul(x1_turn_bank[0:M, 0:H], touch[0:ROWS[t], t, :], w_pair[0:ROWS[t], t, :],
                                           start=(w_pair is wa and t == 0), stop=(w_pair is wb and t == NT - 1))
                    mm.then_inc(touched, 1)
                pe.wait_ge(onehot_done, n + 1)
                pe.wait_ge(tab_hi, n + 1)
                pe.wait_ge(tab_mid, n + 1)
                pe.wait_ge(tab_lo, n + 1)
                for f in range(w):
                    for r in range(rows):
                        mm = pe.matmul(look_bank[n][:, f * 3 * D:(f + 1) * 3 * D], onehot[n][:, r, f, :],
                                       tab_parts[n][:, f, r, :, :], start=(r == 0), stop=(r == rows - 1))
                mm.then_inc(looked_up, 1)
            pe.wait_ge(small_in, 64)
            pe.wait_ge(looked_ok, len(SETS))
            turn(0)
            pe.wait_ge(x3_a, 1)
            pe.wait_ge(x3_b, 1)
            for t in range(NT):
                select_pair(0, 0, t)
            turn_x(0, 0)
            pe.wait_ge(pair_w_split, 2)
            later_blocks(0, False)
            pe.wait_ge(w1_in, 16)
            pe.wait_ge(mlp_in, 16 * 7)

            def chunk(c):
                layer1(c - 1, 3, 0)
                layer1(c - 1, 3, 1)
                turn_x1(c - 1, 2)
                for n in range(2, 5):
                    layer1(c - 1, 3, n)
                turn(c)
                for n in range(5, NT):
                    layer1(c - 1, 3, n)
                contract_d(c - 1, 2, 0)
                pe.wait_ge(x3_a, c + 1)
                pe.wait_ge(x3_b, c + 1)
                select_pair(c, 0, 0)
                contract_d(c - 1, 2, 1)
                turn_x1(c - 1, 3)
                select_pair(c, 0, 1)
                contract_d(c - 1, 2, 2)
                select_pair(c, 0, 2)
                contract_d(c - 1, 2, 3)
                contract_d(c - 1, 3, 0)
                select_pair(c, 0, 3)
                contract_d(c - 1, 3, 1)
                select_pair(c, 0, 4)
                contract_d(c - 1, 3, 2)
                contract_d(c - 1, 3, 3)
                select_pair(c, 0, 5)
                select_pair(c, 0, 6)
                layer2(c - 1, 0, M)
                turn_x(c, 0)
                later_blocks(c, True)

            with pe.Fori(1, NCH - 1) as c:
                chunk(c)
            c = NCH - 1
            chunk(c)
            turn_x1(c, 2)
            for n in range(NT):
                layer1(c, 3, n)
                if n in (3, 5):
                    contract_d(c, 2, (n - 3) // 2)
            contract_d(c, 2, 2)
            contract_d(c, 2, 3)
            turn_x1(c, 3)
            last_mlp1_dense()
            for g in range(NG):
                contract_d(c, 3, g)
            layer2(c, 0, M)
            last_mlp1()
            mlp2(c, True)
            mlp3(c, True)

        @block.vector
        def _(dve):
            def split_rest(c, f0=0):
                n = (M - f0) * D
                dve.wait_ge(chunk_in, c + 1)
                wait(dve, split_mid, c)
                x = emb[:, bass.ds(c * M * D + f0 * D, n)]
                dve.tensor_tensor(rest[:, 0:n], x, upper(x), ALU.subtract).then_inc(split_left, 1)

            def split_lo(c, f0=0):
                n = (M - f0) * D
                dve.wait_ge(split_left, c + 1)
                dve.tensor_tensor(parts[:, 2, f0:M, :].rearrange("b i d -> b (i d)"), rest[:, 0:n], upper(rest[:, 0:n]),
                                  ALU.subtract).then_inc(split_done, 1)

            def one_hot(n):
                f0, w, rows = SETS[n]
                dve.wait_ge(small_ids_ok, n + 1)
                for r in range(rows):
                    last = dve.tensor_scalar(onehot[n][:, r, :, :].rearrange("p w b -> p (w b)"),
                                             small_ids_h[:, f0 * CH:(f0 + w) * CH], row_id[:, n, r:r + 1], None,
                                             ALU.is_equal)
                last.then_inc(onehot_done, 1)

            def table_rest(n):
                dve.wait_ge(tab_hi, n + 1)
                dve.tensor_tensor(tab[n][:, :, :, :], tab[n][:, :, :, :], tab_parts[n][:, :, :, 0, :],
                                  ALU.subtract).then_inc(tab_rest, 1)

            def table_lo(n):
                f0, w, rows = SETS[n]
                dve.wait_ge(tab_rest, n + 1)
                dve.tensor_tensor(tab_parts[n][:, :, :, 2, :].rearrange("p f r d -> p (f r) d"),
                                  flat(tab[n][:, :, :, :]).rearrange("p (n d) -> p n d", d=D),
                                  upper(flat(tab[n][:, :, :, :])).rearrange("p (n d) -> p n d", d=D),
                                  ALU.subtract).then_inc(tab_lo, 1)

            def keep_turned(c):
                dve.wait_ge(turned, 2 * c + 1)
                dve.tensor_copy(x3[:, :, 0:D // 2].rearrange("p b d -> p d b"),
                                turn_bank[0:P3, :].bitcast(BF16).rearrange("p (d b) -> p d b", b=CH)).then_inc(x3_a, 1)

            def round_hi(c, j, t):
                k = NB * c + j
                dve.wait_ge(sq_done, NT * k + t + 1)
                wait(dve, x1_mm, k - 1)
                dve.tensor_copy(prod_hi[0:ROWS[t], j % 2, t, :], prod[0:ROWS[t], t, :]).then_inc(hi_dve, 1)

            def take_lo(c, j, t):
                k = NB * c + j
                if t in DVE_ROUNDS:
                    dve.wait_ge(hi_dve, len(DVE_ROUNDS) * k + DVE_TO[t + 1])
                else:
                    dve.wait_ge(hi_act, (NT - len(DVE_ROUNDS)) * k + ACT_TO[t + 1])
                wait(dve, x1_mm, k - 1)
                rows = slice(0, 128) if t < FULL else slice(32, 64)
                dve.tensor_tensor(prod_lo[:, j % 2, t, :] if t < FULL else prod_hi[rows, j % 2, t, :], prod[rows, t, :],
                                  prod_hi[rows, j % 2, t, :], ALU.subtract).then_inc(lo_done, 1)

            def tiles(c, j, n0, n1):
                for n in range(n0, n1):
                    if n - 1 in DVE_ROUNDS:
                        round_hi(c, j, n - 1)
                    if n >= LAG:
                        take_lo(c, j, n - LAG)

            def take_xs_lo(c, j):
                k = NB * c + j
                dve.wait_ge(xs_hi_done, k + 1)
                x_turned = misc_bank[:, 0:NG * MO].rearrange("p (g i) -> p g i", g=NG)[:, :, 0:M]
                for e in range(2):
                    last = dve.scalar_tensor_tensor(xs[:, 1, :, e, 0:M], x_turned, parity[:, e:e + 1],
                                                    xs[:, 0, :, e, 0:M], ALU.mult, ALU.subtract)
                last.then_inc(xs_lo_done, 1)

            def take_x1_lo(c, j):
                k = NB * c + j
                dve.wait_ge(x1_rounded, k + 1)
                for half in (slice(0, NG // 2 * H), slice(NG // 2 * H, NG * H)):
                    dve.tensor_tensor(x1_lo[:, j % 2, half], x1_turn_bank[:, half], x1_hi[:, j % 2, half],
                                      ALU.subtract).then_inc(x1_done, 1)

            def keep_g(c, j, g):
                k = NB * c + j
                dve.wait_ge(g_mm, NG * k + g + 1)
                dve.tensor_copy(g_sb[:, :, (j * NG + g) * GB:(j * NG + g + 1) * GB],
                                g_bank[g % 2][:, 0:GC].rearrange("p (b i) -> p i b", b=GB)).then_inc(g_dve, 1)

            def relu1(c, last=False):
                for m in range(M1):
                    dve.wait_ge(h1_mm, M1 * c + (m + 1 if last else M1))
                    dve.tensor_scalar(h1[:, m, :], h1_banks[last][m][:, m * CH:(m + 1) * CH], bt1[:, m:m + 1], 0.0,
                                      ALU.add, ALU.max).then_inc(h1_done, 1)

            def later_blocks(c, has_previous, split):
                for j in range(1, NB):
                    if has_previous and j == 2:
                        relu1(c - 1)
                    tiles(c, j, 0, DVE_X1_AT)
                    if j >= 2:
                        take_x1_lo(c, j - 2)
                    if j == NB - 1 and split == "early":
                        split_rest(c + 1)
                    tiles(c, j, DVE_X1_AT, 6)
                    if j >= 2:
                        keep_g(c, j - 2, 1)
                    if j == NB - 1 and split == "early":
                        split_lo(c + 1)
                    tiles(c, j, 6, NT + 1)
                    if j >= 2:
                        keep_g(c, j - 2, 3)
                    tiles(c, j, NT + 1, NT + LAG)
                    if j == NB - 1 and split == "late":
                        split_rest(c + 1)
                        split_lo(c + 1)
                    take_xs_lo(c, j)

            dve.memset(xs[:, :, :, :, :].rearrange("p q g e i -> p (q g e i)").bitcast(F32), 0.0).then_inc(xblk_zero, 1)
            dve.memset(xblk[:, :, :, :, :, :].rearrange("p a q g b i -> p (a q g b i)").bitcast(F32), 0.0).then_inc(xblk_zero, 1)
            dve.wait_ge(row_id_in, 16)
            for n in range(len(SETS)):
                one_hot(n)
                table_rest(n)
                table_lo(n)
            split_rest(0, NS)
            split_lo(0, NS)
            dve.wait_ge(pair_w_in, 48)
            dve.tensor_tensor(pair_w[:, :, :], wa[:, :, :], wb[:, :, :], ALU.add).then_inc(pair_w_sum, 1)
            dve.wait_ge(pair_w_sum, 1)
            dve.wait_ge(touched, 1)
            dve.tensor_tensor(pair_w[0:M, 0, :], pair_w[0:M, 0, :], x1_turn_bank[0:M, 0:H],
                              ALU.subtract).then_inc(pair_w_done, 1)
            dve.wait_ge(small_in, 64)
            dve.wait_ge(xblk_zero, 2)
            dve.tensor_copy(xs[:, 0, :, :, M], parity[:, :].unsqueeze(1).to_broadcast([128, NG, 2])).then_inc(xs_ones, 1)
            keep_turned(0)
            dve.wait_ge(pair_w_split, 1)
            dve.scalar_tensor_tensor(pair_w_lo[:, :, :], pair_w[:, 0:FULL, :], 0.5, pair_w_hi[:, 0:FULL, :], ALU.mult,
                                     ALU.subtract)
            dve.scalar_tensor_tensor(pair_w_hi[64:96, FULL, :], pair_w[64:96, FULL, :], 0.5, pair_w_hi[64:96, FULL, :],
                                     ALU.mult, ALU.subtract).then_inc(pair_w_split, 1)
            tiles(0, 0, 0, NT + LAG)
            take_xs_lo(0, 0)
            later_blocks(0, False, "late")
            dve.wait_ge(mlp_in, 16 * 7)

            def chunk(c, has_next):
                take_x1_lo(c - 1, 2)
                keep_turned(c)
                keep_g(c - 1, 2, 1)
                take_x1_lo(c - 1, 3)
                keep_g(c - 1, 2, 3)
                keep_g(c - 1, 3, 1)
                keep_g(c - 1, 3, 3)
                tiles(c, 0, 0, NT + LAG)
                take_xs_lo(c, 0)
                later_blocks(c, True, "early" if has_next else None)

            with dve.Fori(1, NCH - 1) as c:
                chunk(c, True)
            c = NCH - 1
            chunk(c, False)
            take_x1_lo(c, 2)
            keep_g(c, 2, 1)
            keep_g(c, 2, 3)
            take_x1_lo(c, 3)
            keep_g(c, 3, 1)
            keep_g(c, 3, 3)
            relu1(c, True)

        @block.scalar
        def _(act):
            def keep_turned(c):
                act.wait_ge(turned, 2 * c + 2)
                act.activation(x3[:, :, D // 2:D].rearrange("p b d -> p d b"),
                               misc_bank[0:P3, :].bitcast(BF16).rearrange("p (d b) -> p d b", b=CH),
                               ACT.Copy).then_inc(x3_b, 1)

            def split_first(c, f0=0):
                act.wait_ge(chunk_in, c + 1)
                act.activation(parts[:, 0, f0:M, :].rearrange("b i d -> b (i d)"),
                               upper(emb[:, bass.ds(c * M * D + f0 * D, (M - f0) * D)]), ACT.Copy)

            def split_second(c, f0=0):
                act.wait_ge(split_left, c + 1)
                act.activation(parts[:, 1, f0:M, :].rearrange("b i d -> b (i d)"),
                               upper(rest[:, 0:(M - f0) * D]), ACT.Copy).then_inc(split_mid, 1)

            def square(c, j, t):
                n = NT * (NB * c + j) + t
                act.wait_ge(pair_sel, n + 1)
                wait(act, lo_done, n + 1 - NT)
                act.activation(prod[0:ROWS[t], t, :], pair_bank[(j * NT + t) % 2][0:ROWS[t], :],
                               ACT.Square).then_inc(sq_done, 1)

            def round_hi(c, j, t):
                k = NB * c + j
                act.wait_ge(sq_done, NT * k + t + 1)
                wait(act, x1_mm, k - 1)
                act.activation(prod_hi[0:ROWS[t], j % 2, t, :], prod[0:ROWS[t], t, :], ACT.Copy).then_inc(hi_act, 1)

            def tiles(c, j, n0, n1):
                for n in range(n0, n1):
                    if n < NT:
                        square(c, j, n)
                    if n >= 1 and n - 1 not in DVE_ROUNDS:
                        round_hi(c, j, n - 1)

            def keep_x1h(c, j):
                k = NB * c + j
                act.wait_ge(x1_mm, k + 1)
                wait(act, x1_turned, k)
                act.activation(x1h[:, :], x1_bank[:, :], ACT.Copy).then_inc(x1_kept, 1)

            def keep_x1(c, j):
                k = NB * c + j
                act.wait_ge(x1_turned, k + 1)
                wait(act, g_mm, NG * (k - 1))
                act.activation(x1_hi[:, j % 2, :], x1_turn_bank[:, :], ACT.Copy).then_inc(x1_rounded, 1)

            def round_xs(c, j):
                k = NB * c + j
                act.wait_ge(xt_done, k + 1)
                wait(act, xblk_done, SPREAD * k)
                x_turned = misc_bank[:, 0:NG * MO].rearrange("p (g i) -> p g i", g=NG)[:, :, 0:M]
                for e in range(2):
                    last = act.activation(xs[:, 0, :, e, 0:M], x_turned, ACT.Copy, scale=parity[:, e:e + 1])
                last.then_inc(xs_hi_done, 1)

            def keep_g(c, j, g):
                k = NB * c + j
                act.wait_ge(g_mm, NG * k + g + 1)
                act.activation(g_sb[:, :, (j * NG + g) * GB:(j * NG + g + 1) * GB],
                               g_bank[g % 2][:, 0:GC].rearrange("p (b i) -> p i b", b=GB), ACT.Copy).then_inc(g_act, 1)

            def keep_z2(c):
                act.wait_ge(z2_mm, c + 1)
                act.activation(z2[:, :], turn_bank[:, 0:CH], ACT.Copy).then_inc(z2_done, 1)

            def relu2(c, last=False):
                for m in range(M2):
                    act.wait_ge(h2_mm, M2 * c + (m + 1 if last else M2))
                    act.activation(h2[:, m, :], h2_banks[last][m][:, m * CH:(m + 1) * CH], ACT.Relu,
                                   bias=bt2[:, m:m + 1]).then_inc(h2_done, 1)

            def keep_y(c, last=False):
                act.wait_ge(y_mm, c + 1)
                act.activation(y_sb[:, bass.ds(c * CH, CH)], y_bank[last][0:1, 0:CH], ACT.Copy).then_inc(mlp_through, 1)

            def later_blocks(c, has_previous, split):
                for j in range(1, NB):
                    if j == NB - 1 and split == "early":
                        split_first(c + 1)
                    tiles(c, j, 0, 1)
                    if j >= 2:
                        keep_x1(c, j - 2)
                    tiles(c, j, 1, 3)
                    if has_previous and j == 3:
                        relu2(c - 1)
                    tiles(c, j, 3, 4)
                    if j == NB - 1 and split == "early":
                        split_second(c + 1)
                    if j >= 2:
                        keep_g(c, j - 2, 0)
                    tiles(c, j, 4, 6)
                    if j >= 2:
                        keep_g(c, j - 2, 2)
                    keep_x1h(c, j - 1)
                    tiles(c, j, 6, NT + 1)
                    if j == NB - 1 and split == "late":
                        split_first(c + 1)
                        split_second(c + 1)
                    round_xs(c, j)
                if has_previous:
                    keep_y(c - 1)

            def keep_table_mid(n):
                act.wait_ge(tab_rest, n + 1)
                act.activation(tab_parts[n][:, :, :, 1, :].rearrange("p f r d -> p (f r) d"),
                               upper(flat(tab[n][:, :, :, :])).rearrange("p (n d) -> p n d", d=D),
                               ACT.Copy).then_inc(tab_mid, 1)

            def keep_looked_up(n):
                f0, w, _ = SETS[n]
                act.wait_ge(looked_up, n + 1)
                act.activation(parts[:, :, f0:f0 + w, :],
                               look_bank[n][:, 0:w * 3 * D].rearrange("b (f q d) -> b q f d", q=3, d=D),
                               ACT.Copy).then_inc(looked_ok, 1)

            act.sem_inc(mlp_through, 1)
            for n, (f0, w, rows) in enumerate(SETS):
                act.wait_ge(small_ids_in[n], 16)
                act.activation(small_ids_h[:, f0 * CH:(f0 + w) * CH], small_ids_i[:, f0 * CH:(f0 + w) * CH],
                               ACT.Copy).then_inc(small_ids_ok, 1)
                act.wait_ge(tab_in[n], 16)
                act.activation(tab_parts[n][:, :, :, 0, :], tab[n][:, :, :, :], ACT.Copy).then_inc(tab_hi, 1)
                if n:
                    keep_table_mid(n - 1)
            keep_looked_up(0)
            keep_looked_up(1)
            keep_table_mid(2)
            split_first(0, NS)
            split_second(0, NS)
            keep_looked_up(2)
            keep_turned(0)
            act.wait_ge(pair_w_done, 1)
            act.activation(pair_w_hi[:, :, :], pair_w[:, :, :], ACT.Copy, scale=0.5).then_inc(pair_w_split, 1)
            tiles(0, 0, 0, NT + 1)
            round_xs(0, 0)
            later_blocks(0, False, "late")
            act.wait_ge(mlp_in, 16 * 7)

            def chunk(c, has_next):
                keep_x1(c - 1, 2)
                keep_turned(c)
                keep_x1h(c - 1, 3)
                keep_g(c - 1, 2, 0)
                square(c, 0, 0)
                keep_x1(c - 1, 3)
                keep_g(c - 1, 2, 2)
                square(c, 0, 1)
                square(c, 0, 2)
                keep_g(c - 1, 3, 0)
                square(c, 0, 3)
                keep_g(c - 1, 3, 2)
                square(c, 0, 4)
                for t in range(4):
                    if t not in DVE_ROUNDS:
                        round_hi(c, 0, t)
                tiles(c, 0, 5, NT + 1)
                keep_z2(c - 1)
                round_xs(c, 0)
                later_blocks(c, True, "early" if has_next else None)

            with act.Fori(1, NCH - 1) as c:
                chunk(c, True)
            c = NCH - 1
            chunk(c, False)
            keep_x1(c, 2)
            keep_g(c, 2, 0)
            keep_g(c, 2, 2)
            keep_x1h(c, 3)
            keep_x1(c, 3)
            keep_g(c, 3, 0)
            keep_g(c, 3, 2)
            keep_z2(c)
            relu2(c, True)
            keep_y(c, True)


def kernel(**inputs):
    import ml_dtypes
    import numpy as np
    import concourse.bacc as bacc
    from concourse.bass_utils import run_bass_kernel_spmd

    nc = bacc.Bacc("TRN2", target_bir_lowering=False, num_devices=1)
    arrays, args = {}, []

    def give(name, a):
        arrays[name] = np.ascontiguousarray(a)
        args.append(nc.dram_tensor(name, arrays[name].shape, mybir.dt.from_np(arrays[name].dtype),
                                   kind="ExternalInput").ap())
        return args.pop()

    x = {n: np.asarray(a) for n, a in inputs.items()}
    by_field = x["ids"][:, ORDER]
    ids = give("ids", by_field.reshape(NCH, CH, M).transpose(1, 0, 2).reshape(CH, NCH * M))
    tables = [give(f"tbl_{f}", x[f"tbl_{f}"]) for f in ORDER]
    small_tables = [give(f"small_{n}", np.stack([x[f"tbl_{f}"] for f in ORDER[f0:f0 + w]]))
                    for n, (f0, w, _) in enumerate(SETS)]
    small_ids = give("small_ids", by_field[:CH, :NS].T.reshape(1, NS * CH))
    row_ids = np.zeros((SP, len(SETS), 10), np.float32)
    for n, (_, _, rows) in enumerate(SETS):
        row_ids[:, n, :rows] = np.arange(SP * rows).reshape(SP, rows)
    row_ids = give("row_ids", row_ids)

    i, j = np.triu_indices(M, 1)
    i, j = np.concatenate([np.arange(M), i]), np.concatenate([np.arange(M), j])
    at = np.array(ORDER)
    w0 = x["L0_rec_W0"][0]
    w_a, w_b = np.zeros((2, NT, 128, H), np.float32)
    touches = np.zeros((NT, 128, M), np.float32)
    select = np.zeros((3, M, NT, 128), np.float32)
    for copy in range(3):
        n = np.arange(128 * FULL if copy else 0, PAIRS)
        t, r = n // 128, n % 128 + 32 * copy
        w_a[t, r], w_b[t, r] = w0[at[i[n]] * M + at[j[n]]], w0[at[j[n]] * M + at[i[n]]]
        select[:, i[n], t, r] = 1.0
        select[:, j[n], t, r] = 1.0
    n = np.arange(M, PAIRS)
    touches[n // 128, n % 128, i[n]] = 1.0
    touches[n // 128, n % 128, j[n]] = 1.0
    pair_w_a = give("pair_w_a", w_a.transpose(1, 0, 2))
    pair_w_b = give("pair_w_b", w_b.transpose(1, 0, 2))
    sel = give("select", select.reshape(P3, NT, 128).astype(ml_dtypes.bfloat16))
    touches = give("touches", touches.transpose(1, 0, 2))
    w1 = give("w1", x["L0_rec_W1"][0].reshape(M, H, H)[ORDER].reshape(M * H, H))
    w_top1 = give("w_top1", x["W_top1"][:2 * H])
    w_dense = give("w_dense", x["W_top1"][2 * H:])
    b_top1 = give("b_top1", x["b_top1"].reshape(M1, 128).T)
    w_top2 = give("w_top2", x["W_top2"])
    b_top2 = give("b_top2", x["b_top2"].reshape(M2, 128).T)
    w_top3 = give("w_top3", x["W_top3"].reshape(M2, 128).T)
    dense_t = give("dense_t", x["dense_ctx"].T)
    ident_f = give("ident_f", np.eye(128, dtype=np.float32))
    ident_b = give("ident_b", np.eye(128, dtype=ml_dtypes.bfloat16))
    parity_row = give("parity_row", np.tile(np.repeat(np.eye(2, dtype=np.float32), D, axis=0), (GB // 2, 1)))
    y = nc.dram_tensor("y", (1, B), F32, kind="ExternalOutput").ap()
    build_tower(nc, ids, tables, pair_w_a, pair_w_b, touches, sel, w1, w_top1, w_dense, b_top1, w_top2, b_top2, w_top3,
                dense_t, ident_b, ident_f, parity_row, small_ids, row_ids, small_tables, y)
    result = run_bass_kernel_spmd(nc, [arrays], core_ids=[0])
    return np.asarray(result.results[0]["y"]).reshape(B, 1)
```
